# Optimizing a Trainium2 kernel written in Bass

```python
import numpy as np
import jax
import jax.numpy as jnp

def _softmax(x, axis=-1):
    return jax.nn.softmax(x, axis=axis)

def _gelu(x):
    return jax.nn.gelu(x, approximate=True)

def _silu(x):
    return jax.nn.silu(x)

def _sigmoid(x):
    return jax.nn.sigmoid(x)

def _layernorm(x, axis=-1, eps=1e-05):
    m = jnp.mean(x, axis=axis, keepdims=True)
    v = jnp.var(x, axis=axis, keepdims=True)
    return (x - m) / jnp.sqrt(v + eps)

def _scatter_add(tgt, idx, src, axis=0):
    return tgt.at[idx].add(src)

def _segment_sum(src, seg, n):
    return jax.ops.segment_sum(src, seg, n)
kernel_name = 'mk_gnn_preln_d2_gnn_r32_e559c8'

def setup_inputs(seed: int=0):
    np.random.seed(seed)
    _w = jnp.asarray

    def _rec_inputs():
        import jax
        import jax.numpy as jnp
        _gk = jax.random.key(seed)
        x = -0.0003929 + 0.9999 * jax.random.normal(jax.random.fold_in(_gk, 1), (512, 1024), jnp.float32)
        src = jax.random.randint(jax.random.fold_in(_gk, 2), (8192,), 0, 512, jnp.int32)
        dst = jax.random.randint(jax.random.fold_in(_gk, 3), (8192,), 0, 512, jnp.int32)
        _o = jnp.argsort(dst, stable=True)
        src = src[_o]
        dst = dst[_o]
        edge_weight = jax.random.uniform(jax.random.fold_in(_gk, 12), (8192,), jnp.float32, 0.0, 0.999994)
        return (x, src, dst, edge_weight)
    x, src, dst, edge_weight = _rec_inputs()

    def _L0_gnn_setup():
        import jax, jax.numpy as jnp
        import numpy as np
        NH, NO = (128, 384)
        N = NH + NO
        E_HH, E_OO, E_HO = (256, 1280, 512)
        E = E_HH + E_OO + E_HO
        D = 1024
        key = jax.random.key(seed)
        ks = jax.random.split(key, 12)
        w = lambda k, s: jax.random.normal(k, s, jnp.float32) * 0.02
        return {'n_f': jax.random.normal(ks[0], (N, D), jnp.float32), 'W_hh': w(ks[1], (2 * D, D)), 'b_hh': jnp.zeros((D,), jnp.float32), 'W_oo': w(ks[2], (2 * D, D)), 'b_oo': jnp.zeros((D,), jnp.float32), 'W_ho': w(ks[3], (2 * D, D)), 'b_ho': jnp.zeros((D,), jnp.float32), 'W_a': w(ks[4], (D, 1)), 'b_a': jnp.zeros((1,), jnp.float32), 'W_hn': w(ks[5], (2 * D, D)), 'b_hn': jnp.zeros((D,), jnp.float32), 'W_on': w(ks[6], (2 * D, D)), 'b_on': jnp.zeros((D,), jnp.float32), 'edge_src': jax.random.randint(ks[7], (E,), 0, N, jnp.int32), 'edge_dst': jax.random.randint(ks[8], (E,), 0, N, jnp.int32)}
    _L0_gnn_all = _L0_gnn_setup()
    _L0_gnn_in = {k: v for k, v in _L0_gnn_all.items() if k in ('W_hh', 'b_hh', 'W_oo', 'b_oo', 'W_ho', 'b_ho', 'W_a', 'b_a', 'W_hn', 'b_hn', 'W_on', 'b_on')}
    del _L0_gnn_all

    def _L1_gnn_setup():
        import jax, jax.numpy as jnp
        import numpy as np
        N_NODES = 512
        N_EDGES = 4096
        D = 1024
        key = jax.random.key(seed)
        k_x, k_w, k_W, k_s, k_d = jax.random.split(key, 5)
        x = jax.random.normal(k_x, (N_NODES, D), dtype=jnp.float32)
        edge_w = jax.random.uniform(k_w, (N_EDGES,), dtype=jnp.float32)
        W = jax.random.normal(k_W, (D, D), dtype=jnp.float32) * (1.0 / np.sqrt(D))
        b = jnp.zeros((D,), dtype=jnp.float32)
        src = jax.random.randint(k_s, (N_EDGES,), 0, N_NODES)
        dst = jax.random.randint(k_d, (N_EDGES,), 0, N_NODES)
        return {'x': x, 'edge_w': edge_w, 'W': W, 'b': b, 'src': src, 'dst': dst}
    _L1_gnn_all = _L1_gnn_setup()
    _L1_gnn_in = {k: v for k, v in _L1_gnn_all.items() if k in ('W', 'b')}
    del _L1_gnn_all
    return {'x': x, 'src': src, 'dst': dst, 'edge_weight': edge_weight, 'L0_gnn_W_hh': _L0_gnn_in['W_hh'], 'L0_gnn_b_hh': _L0_gnn_in['b_hh'], 'L0_gnn_W_oo': _L0_gnn_in['W_oo'], 'L0_gnn_b_oo': _L0_gnn_in['b_oo'], 'L0_gnn_W_ho': _L0_gnn_in['W_ho'], 'L0_gnn_b_ho': _L0_gnn_in['b_ho'], 'L0_gnn_W_a': _L0_gnn_in['W_a'], 'L0_gnn_b_a': _L0_gnn_in['b_a'], 'L0_gnn_W_hn': _L0_gnn_in['W_hn'], 'L0_gnn_b_hn': _L0_gnn_in['b_hn'], 'L0_gnn_W_on': _L0_gnn_in['W_on'], 'L0_gnn_b_on': _L0_gnn_in['b_on'], 'L1_gnn_W': _L1_gnn_in['W'], 'L1_gnn_b': _L1_gnn_in['b']}

def reference(x, src, dst, edge_weight, L0_gnn_W_hh, L0_gnn_b_hh, L0_gnn_W_oo, L0_gnn_b_oo, L0_gnn_W_ho, L0_gnn_b_ho, L0_gnn_W_a, L0_gnn_b_a, L0_gnn_W_hn, L0_gnn_b_hn, L0_gnn_W_on, L0_gnn_b_on, L1_gnn_W, L1_gnn_b):
    import jax
    import jax.numpy as jnp

    def _L0_gnn_ref(n_f, W_hh, b_hh, W_oo, b_oo, W_ho, b_ho, W_a, b_a, W_hn, b_hn, W_on, b_on, edge_src, edge_dst):
        import jax, jax.numpy as jnp
        import numpy as np
        NH, NO = (128, 384)
        N = NH + NO
        E_HH, E_OO, E_HO = (256, 1280, 512)
        E = E_HH + E_OO + E_HO
        D = 1024
        feat = jnp.concatenate([n_f[edge_src], n_f[edge_dst]], axis=1)
        e_hh = jax.nn.relu(feat[:E_HH] @ W_hh + b_hh)
        e_oo = jax.nn.relu(feat[E_HH:E_HH + E_OO] @ W_oo + b_oo)
        e_ho = jax.nn.relu(feat[E_HH + E_OO:] @ W_ho + b_ho)
        e_f = jnp.concatenate([e_hh, e_oo, e_ho], axis=0)
        logit = (e_f @ W_a + b_a)[:, 0]
        m = jax.lax.stop_gradient(jax.ops.segment_max(logit, edge_dst, num_segments=N))
        ex = jnp.exp(logit - m[edge_dst])
        den = jax.ops.segment_sum(ex, edge_dst, num_segments=N)
        alpha = ex / den[edge_dst]
        z_f = jax.ops.segment_sum(alpha[:, None] * n_f[edge_src], edge_dst, num_segments=N)
        nf2 = jnp.concatenate([n_f, z_f], axis=1)
        h_new = jax.nn.relu(nf2[:NH] @ W_hn + b_hn)
        o_new = jax.nn.relu(nf2[NH:] @ W_on + b_on)
        return jnp.concatenate([h_new, o_new], axis=0)

    def _L1_gnn_ref(x, edge_w, W, b, src, dst):
        import jax, jax.numpy as jnp
        import numpy as np
        N_NODES = 512
        N_EDGES = 4096
        D = 1024
        "EdgeWeightNorm(norm='both') -> GraphConv(norm='both', weight, bias) -> ReLU.\n\n            Matches DGL semantics:\n              c_ij   = w_ij / sqrt(sum_out_w[src] * sum_in_w[dst])   (EdgeWeightNorm 'both')\n              h_j    = relu( D_in[j]^-1/2 * sum_i c_ij * D_out[i]^-1/2 * x_i  @ W + b )\n            where D_out/D_in are structural degrees clamped to >= 1.\n            "
        n = x.shape[0]
        ones = jnp.ones_like(edge_w)
        w_out = jax.ops.segment_sum(edge_w, src, num_segments=n)
        w_in = jax.ops.segment_sum(edge_w, dst, num_segments=n)
        c = edge_w * jax.lax.rsqrt(w_out[src] * w_in[dst])
        deg_out = jnp.clip(jax.ops.segment_sum(ones, src, num_segments=n), 1.0)
        deg_in = jnp.clip(jax.ops.segment_sum(ones, dst, num_segments=n), 1.0)
        xs = x * jax.lax.rsqrt(deg_out)[:, None]
        msg = xs[src] * c[:, None]
        agg = jax.ops.segment_sum(msg, dst, num_segments=n)
        agg = agg * jax.lax.rsqrt(deg_in)[:, None]
        return jax.nn.relu(agg @ W + b)
    h = jnp.maximum(_layernorm(x, axis=-1), 0.0)
    x = x + _L0_gnn_ref(h, L0_gnn_W_hh, L0_gnn_b_hh, L0_gnn_W_oo, L0_gnn_b_oo, L0_gnn_W_ho, L0_gnn_b_ho, L0_gnn_W_a, L0_gnn_b_a, L0_gnn_W_hn, L0_gnn_b_hn, L0_gnn_W_on, L0_gnn_b_on, src, dst)
    h = jnp.maximum(_layernorm(x, axis=-1), 0.0)
    x = x + _L1_gnn_ref(h, edge_weight, L1_gnn_W, L1_gnn_b, src, dst)
    return x

_drawn_inputs = setup_inputs


def setup_inputs(seed=0):
    import zlib

    import numpy as np

    out = dict(_drawn_inputs(seed))
    spreads = {'L0_gnn_b_hh': (0.0, 2.0),
     'L0_gnn_b_oo': (0.0, 2.0),
     'L0_gnn_b_ho': (0.0, 0.8),
     'L0_gnn_b_hn': (0.0, 0.1),
     'L0_gnn_b_on': (0.0, 0.1),
     'L1_gnn_b': (0.0, 0.1)}
    factors = {'edge_weight': 38.599,
     'L0_gnn_W_hh': 8.0,
     'L0_gnn_W_oo': 8.0,
     'L0_gnn_W_ho': 6.522,
     'L0_gnn_W_a': 6.174,
     'L1_gnn_W': 3.171}
    for name, (base, spread) in spreads.items():
        noise = np.random.default_rng([zlib.crc32(name.encode()), seed]).standard_normal(out[name].shape)
        drawn = base * np.exp(spread * noise) if base else spread * noise
        out[name] = jnp.asarray(drawn.astype(out[name].dtype))
    for name, factor in factors.items():
        out[name] = (out[name] * factor).astype(out[name].dtype)
    return out
```

```python
from contextlib import ExitStack

import concourse.bass as bass
from concourse import mybir
from concourse.alu_op_type import AluOpType as ALU

ACT = mybir.ActivationFunctionType
AX = mybir.AxisListType
F32, F32R, BF16, F16 = mybir.dt.float32, mybir.dt.float32r, mybir.dt.bfloat16, mybir.dt.float16
F8, I32 = mybir.dt.float8e4, mybir.dt.int32

P = 128
EPS = 1e-5
TINY = 1e-30
BIG = float(2 ** 20)

TILE_HH, TILE_OO = 2, 12
BLOCK_H = 1


def tile_order(T):
    first = 16
    runs = [(0, first, T - first)]
    runs.append((T - first, TILE_OO, first - TILE_OO))
    runs.append((T - TILE_OO, TILE_HH, TILE_OO - TILE_HH))
    runs.append((T - TILE_HH, 0, TILE_HH))
    return runs


class Step:

    def __init__(self, eng, sem):
        self.eng, self.sem, self.n = eng, sem, 0

    def __call__(self, ins):
        self.n += 1
        ins.then_inc(self.sem, 1)
        self.eng.wait_ge(self.sem, self.n)


def build(nc, x, src, dst, edge_w, W_hh, b_hh, W_oo, b_oo, W_ho, b_ho, W_a, b_a, W_hn, b_hn, W_on, b_on,
          W_1, b_1, out):
    N, D = x.shape
    E = src.shape[0]
    B, K, T = N // P, D // P, E // P
    H = D // 2
    CT = 8
    NC = T // CT
    CE = CT * P
    RUNS = tile_order(T)
    kind_of = lambda i: 0 if i < T - TILE_OO else (1 if i < T - TILE_HH else 2)

    kinds = [(W_ho, b_ho), (W_oo, b_oo), (W_hh, b_hh)]
    UNITS = 2 * len(kinds)
    C_TOP = K * UNITS
    C_BOT = C_TOP + 2 * K
    C_L1 = C_BOT + 2 * K
    C_END = C_L1 + K

    def chunk_rows(c):
        if c < C_TOP:
            u, k = c // K, c % K
            w, row = kinds[u // 2][0], (u % 2) * D + k * P
        elif c < C_L1:
            q, k = (c - C_TOP) // K, c % K
            w, row = (W_on, W_hn)[q % 2], (q // 2) * D + k * P
        else:
            w, row = W_1, (c - C_L1) * P
        return w[row:row + P, :]

    with ExitStack() as ctx:
        place = [(nc.sbuf_base + 31) // 32 * 32]
        size = {F32: 4, F32R: 4, I32: 4, BF16: 2, F16: 2, F8: 1}

        def sb(name, shape, dt, over=None):
            n = size[dt]
            for d in shape[1:]:
                n *= d
            at = place[0] if over is None else over
            t = nc.alloc_sbuf_tensor_at(name, shape, dt, offset=at)
            if over is None:
                place[0] += (n + 31) // 32 * 32
                assert place[0] <= nc.sbuf_usable_end, (name, place[0])
            return t, at

        def sem(name):
            return ctx.enter_context(nc.semaphore(name))

        banks = ctx.enter_context(nc.psum_tensor("banks", [P, 8 * H], F32))
        bank = [banks[:, i * H:(i + 1) * H] for i in range(8)]

        xf, _ = sb("xf", [P, B, D], F32)
        fT_hi, _ = sb("fT_hi", [P, K, N], F32R)
        fT_lo, _ = sb("fT_lo", [P, K, N], F32R)
        w_raw, _ = sb("w_raw", [P, 2, D], F32)
        w_hi, _ = sb("w_hi", [P, 4, D], F32R)
        w_lo, _ = sb("w_lo", [P, 4, D], F32R)
        member, at = sb("member", [P, B, E], BF16)
        hn_hi, _ = sb("hn_hi", [P, B, D], F32R, over=at)
        hn_lo, _ = sb("hn_lo", [P, B, D], F32R, over=at + B * D * 4)
        hf, _ = sb("hf", [P, B, D], F32, over=at + 2 * B * D * 4)
        adjwT, _ = sb("adjwT", [P, B, N], F32, over=at + 3 * B * D * 4)
        rows, at = sb("rows", [P, 4, D], F32)
        dst_rep, _ = sb("dst_rep", [P, 4, CE], I32, over=at)
        adjT_hi, _ = sb("adjT_hi", [P, B, N], F32R, over=at)
        adjT_lo, _ = sb("adjT_lo", [P, B, N], F32R, over=at + B * N * 4)
        stage, at = sb("stage", [P, 4, H], F32)
        adj, _ = sb("adj", [P, B, N], F32, over=at)
        pick_dst1, _ = sb("pick_dst1", [P, 2, 3, N], BF16, over=at)
        pick_src1, _ = sb("pick_src1", [P, 2, N], BF16, over=at + 2 * 3 * N * 2)
        wa_rep, _ = sb("wa_rep", [P, D], F32)
        bias, _ = sb("bias", [P, 2, D], F32)
        lift, at = sb("lift", [P, CE], F32)
        ids_row, _ = sb("ids_row", [T, 2, P], I32, over=at)
        ids_rowf, _ = sb("ids_rowf", [T, 3, P], F32, over=at + 2 * P * 4)
        masked, at = sb("masked", [P, CE // 2], BF16)
        e_part, _ = sb("e_part", [P, 3, T], F32, over=at)
        pair_row, _ = sb("pair_row", [1, 3, T // 2], F32, over=at)
        nibble, _ = sb("nibble", [1, T // 8, 4], F32, over=at + 3 * T // 2 * 4)
        pick_src0, _ = sb("pick_src0", [P, 2, N], BF16)
        pick_dst0, _ = sb("pick_dst0", [P, 2, 3, N], BF16)
        pick_src, pick_dst = (pick_src0, pick_src1), (pick_dst0, pick_dst1)
        ident, _ = sb("ident", [P, P], F32)
        node_no, _ = sb("node_no", [P, N], F16)
        zeros, _ = sb("zeros", [P, P], BF16)
        ids_f, _ = sb("ids_f", [P, 3, T], F32)
        ids_i, _ = sb("ids_i", [P, 2, T], I32)
        node_id, _ = sb("node_id", [P, B], F32)
        w_part, _ = sb("w_part", [P, 3, T], F32)
        tile_lo, _ = sb("tile_lo", [T, 2], F32)
        pair_word, _ = sb("pair_word", [1, T // 8], I32)
        part16, _ = sb("part16", [P, T], BF16)
        rest, _ = sb("rest", [P, T], F32)
        logit, at = sb("logit", [P, T], F32)
        ex, _ = sb("ex", [P, T], F32, over=at)
        lb, _ = sb("lb", [P, T], F32)
        lifted, _ = sb("lifted", [P, 2, 32], F32)
        liftT, _ = sb("liftT", [P, 2, 32], F32)
        me, _ = sb("me", [P, T], F32)
        ba_rep, _ = sb("ba_rep", [P, 1], F32)
        ones_f, _ = sb("ones_f", [P, 1], F32)
        ones_b, _ = sb("ones_b", [P, 1], BF16)
        nhalf, _ = sb("nhalf", [P, B], F32)
        stats, _ = sb("stats", [P, B, 2, 6], F32)
        mv, _ = sb("mv", [P, B, 2], F32)
        veps, _ = sb("veps", [P, B], F32)
        rstd, _ = sb("rstd", [P, B], F32)
        count, _ = sb("count", [P, B, NC], F32)
        cmax, _ = sb("cmax", [P, B, 2 * NC], F32)
        deg_in, _ = sb("deg_in", [P, B], F32)
        deg_out, _ = sb("deg_out", [P, B], F32)
        wsum, _ = sb("wsum", [P, B], F32)
        w_out, _ = sb("w_out", [P, B], F32)
        f_dst, _ = sb("f_dst", [P, B], F32)
        f_src, _ = sb("f_src", [P, B], F32)
        rden, _ = sb("rden", [P, B], F32)
        mx, _ = sb("mx", [P, B], F32)
        mrest, _ = sb("mrest", [P, B], F32)
        mpart, _ = sb("mpart", [P, B, 3], BF16)

        table = [[nc.dram_tensor(f"table{k}{s}", [N, D], F32, kind="Internal").ap() for s in range(2)]
                 for k in range(3)]
        h_row = nc.dram_tensor("h_row", [N, D], F32, kind="Internal").ap()
        lift_row = nc.dram_tensor("lift_row", [NC, CT, P], F32, kind="Internal").ap()

        h_out = sem("h_out"); h_back = sem("h_back")
        words_ready = sem("words_ready"); x_in = [sem(f"x_in{b}") for b in range(B)]
        ids_in = sem("ids_in"); wa_in = sem("wa_in")
        dst_in = [sem(f"dst_in{s}") for s in range(4)]
        bias_in = [sem(f"bias_in{s}") for s in range(2)]
        w_in = [sem(f"w_in{s}") for s in range(2)]
        stored = [sem(f"stored{s}") for s in range(4)]
        row_in = [sem(f"row_in{s}") for s in range(4)]
        hi_done = sem("hi_done"); lo_done = sem("lo_done"); chunk_used = sem("chunk_used")
        bank_done = sem("bank_done"); evac = sem("evac")
        consts = sem("consts"); own = sem("dve_step"); consts2 = sem("pool_consts_own")
        idsf_ready = sem("idsf_ready"); idsT_ready = sem("idsT_ready"); ids_ready = sem("ids_ready")
        var_ready = sem("var_ready"); rstd_ready = sem("rstd_ready")
        h_pre = sem("h_pre"); h_ready = sem("h_ready"); hT_ready = sem("hT_ready")
        fT_hi_done = sem("fT_hi_done"); fT_lo_done = sem("fT_lo_done")
        member_done = sem("member_done"); edge_done = sem("edge_done")
        lift_ready = sem("lift_ready"); lift_out = sem("lift_out"); lift_in = sem("lift_in"); max_done = sem("max_done")
        src_ready = sem("src_ready"); dst_ready = sem("dst_ready"); adj_done = sem("adj_done"); adj_full = sem("adj_full")
        adj_ready = sem("adj_ready"); adjT_done = sem("adjT_done"); adjwT_ready = sem("adjwT_ready")
        wout_done = sem("wout_done"); wsum_ready = sem("wsum_ready"); wdeg_ready = sem("wdeg_ready"); fac_ready = sem("fac_ready")
        mpart_ready = sem("mpart_ready"); me_done = sem("me_done"); arg_ready = sem("arg_ready"); ex_ready = sem("ex_ready")
        adjT_hi_done = sem("adjT_hi_done"); adjT_lo_done = sem("adjT_lo_done")
        hn_hi_done = sem("hn_hi_done"); hn_lo_done = sem("hn_lo_done")
        z_done = sem("z_done"); x_again = sem("x_again")
        x2_step = sem("x2_step"); t_ready = sem("t_ready"); out_ready = sem("out_ready")
        out_stored = [sem(f"out_stored{s}") for s in range(4)]

        def bank_ready(eng, unit, j):
            halves = unit in (UNITS, UNITS + 1)
            seen = 7 * unit - max(0, unit - UNITS) + (((j - 2) % 8) if halves else j)
            if unit == UNITS + 2:
                seen = 7 * UNITS + 2 * 6 + j
            first_chunk = K * unit + K * max(0, unit - UNITS)
            if halves and j == 1:
                eng.wait_ge(chunk_used, first_chunk + 2 * K)
            elif j == 7:
                eng.wait_ge(chunk_used, first_chunk + K)
            else:
                eng.wait_ge(bank_done, seen + (0 if halves and j == 0 else 1))

        block = ctx.enter_context(nc.Block())
        AB = ((0, 0), (0, 1), (1, 0))
        fT, wS, hn, adjT = (fT_hi, fT_lo), (w_hi, w_lo), (hn_hi, hn_lo), (adjT_hi, adjT_lo)

        @block.sync
        def _(sp):
            for b in range(B):
                sp.dma_start(xf[:, b, :], x[b * P:(b + 1) * P, :]).then_inc(x_in[b], 16)
            for a, arr in enumerate((src, dst, edge_w)):
                tgt = ids_row[:, a, :] if a < 2 else ids_rowf[:, a, :]
                for i0, t0, n in RUNS:
                    sp.dma_start(tgt[i0:i0 + n], arr[t0 * P:(t0 + n) * P].rearrange("(t p) -> t p", p=P)).then_inc(ids_in, 16)

            def load(c):
                if c >= 2:
                    sp.wait_ge(lo_done, c - 1)
                sp.dma_start(w_raw[:, c % 2, :], chunk_rows(c)).then_inc(w_in[c % 2], 16)

            def load_bias(n, vec):
                sp.dma_start(bias[:, n % 2, :], vec.partition_broadcast(P)).then_inc(bias_in[n % 2], 16)

            load(0)
            load(1)
            sp.dma_start(wa_rep[:, :], W_a.rearrange("d o -> (d o)").partition_broadcast(P)).then_inc(wa_in, 16)
            sp.dma_start(ba_rep[:, :], b_a.partition_broadcast(P)).then_inc(wa_in, 16)
            load_bias(0, b_ho)
            load_bias(1, b_oo)
            sp.wait_ge(h_ready, B)
            sp.dma_start(h_row.rearrange("(b p) d -> p b d", p=P), xf[:, :, :]).then_inc(h_out, 16)
            for c in range(2, K + 6):
                load(c)
            for u in range(UNITS):
                for j in range(8):
                    e = 8 * u + j
                    sp.wait_ge(evac, e + 1)
                    m, n = j // 2, j % 2
                    sp.dma_start(table[u // 2][u % 2][m * P:(m + 1) * P, n * H:(n + 1) * H],
                                 stage[:, e % 4, :]).then_inc(stored[e % 4], 16)
                if u % 2 == 1:
                    load_bias(2 + u // 2, (b_hh, b_on, b_hn)[u // 2])
                for c in range(K * (u + 1) + 6, K * (u + 2) + 6):
                    load(c)
            for c in range(C_TOP + 6 + K, C_BOT + 4):
                load(c)
            sp.wait_ge(evac, 8 * UNITS + 8)
            load_bias(5, b_1)
            sp.wait_ge(me_done, 1)
            sp.dma_start(hf[:, :, :], h_row.rearrange("(b p) d -> p b d", p=P)).then_inc(h_back, 16)
            sp.wait_ge(hn_lo_done, B)
            for c in range(C_BOT + 4, C_BOT + 6):
                load(c)
            for b in range(B):
                sp.dma_start(hf[:, b, :], x[b * P:(b + 1) * P, :]).then_inc(x_again, 16)
            for c in range(C_BOT + 6, C_END):
                load(c)
            for j in range(8):
                m, n = j // 2, j % 2
                sp.wait_ge(out_ready, j + 1)
                sp.dma_start(out[m * P:(m + 1) * P, n * H:(n + 1) * H], stage[:, j % 4, :]).then_inc(out_stored[j % 4], 16)
            for s in range(4):
                sp.wait_ge(out_stored[s], 32)

        @block.gpsimd
        def _(pool):
            pool.memset(ident[:, :], 0.0).then_inc(consts2, 1)
            pool.iota(node_no[:, :], [[1, N]], base=0, channel_multiplier=0,
                      allow_small_or_imprecise_dtypes=True).then_inc(consts, 1)
            pool.iota(node_id[:, :], [[P, B]], base=0, channel_multiplier=1,
                      allow_small_or_imprecise_dtypes=True).then_inc(consts, 1)
            pool.memset(ones_f[:, :], 1.0).then_inc(consts, 1)
            pool.memset(ones_b[:, :], 1.0).then_inc(consts, 1)
            pool.memset(zeros[:, :], 0.0).then_inc(consts, 1)
            pool.memset(nhalf[:, :], -0.5).then_inc(consts, 1)
            pool.wait_ge(consts2, 1)
            pool.affine_select(out=ident[:, :], in_=ident[:, :], compare_op=ALU.not_equal, fill=1.0, base=0,
                               pattern=[[-1, P]], channel_multiplier=1).then_inc(consts, 1)
            pool.wait_ge(consts, 7)

            def power(n, dst_t, src_t, ready, done):
                pool.wait_ge(ready, n)
                pool.tensor_tensor(dst_t[:, :], src_t[:, :], nhalf[:, :], ALU.pow).then_inc(done, 1)

            power(1, rstd, veps, var_ready, rstd_ready)
            pool.wait_ge(ids_ready, 1)

            def fetch_src(i, kind, s, lap):
                pool.indirect_dma_start(out=rows[:, s, :], out_offset=None, in_=table[kind][0],
                                        in_offset=bass.IndirectOffsetOnAxis(ap=ids_i[:, 0, i:i + 1], axis=0)
                                        ).then_inc(row_in[s], 16)

            def add_dst(i, kind, s, lap):
                pool.wait_ge(row_in[s], lap * 32 + 16)
                pool.indirect_dma_start(out=rows[:, s, :], out_offset=None, in_=table[kind][1],
                                        in_offset=bass.IndirectOffsetOnAxis(ap=ids_i[:, 1, i:i + 1], axis=0),
                                        compute_op=ALU.add).then_inc(row_in[s], 16)

            def tables_stored(kind):
                for s in range(4):
                    pool.wait_ge(stored[s], 16 * 4 * (kind + 1))

            def pick(g, first_pair):
                if g % 2 == 0 and first_pair + g // 2 >= 2:
                    pool.wait_ge(adj_done, first_pair + g // 2 - 1)
                pool.tensor_scalar(pick_src[g // 2 % 2][:, g % 2, :], node_no[:, :], ids_f[:, 0, g:g + 1], None,
                                   ALU.is_equal).then_inc(src_ready, 1)

            tables_stored(0)
            AHEAD = 2

            def step(i):
                j = i + AHEAD
                if j < T:
                    if kind_of(j) != kind_of(j - 1):
                        tables_stored(kind_of(j))
                    if j >= 4:
                        pool.wait_ge(edge_done, j - 3)
                    fetch_src(j, kind_of(j), j % 4, j // 4)
                add_dst(i, kind_of(i), i % 4, i // 4)

            for i in range(AHEAD):
                fetch_src(i, 0, i, 0)
            MIX = 40
            for i in range(MIX):
                step(i)
            for q in range((T - MIX) // 4):
                for i in range(4):
                    step(MIX + 4 * q + i)
                    for g in range(8 * q + 2 * i, 8 * q + 2 * i + 2):
                        if g == 2:
                            for s in range(4):
                                pool.wait_ge(stored[s], 2 * 16 * UNITS)
                        pick(g, 0)
            first = 2 * (T - MIX)
            for g in range(first, T):
                pick(g, 0)
            power(1, f_dst, wsum, wsum_ready, fac_ready)
            power(1, f_src, w_out, wdeg_ready, fac_ready)
            for g in range(T):
                if g == 2:
                    pool.wait_ge(adjT_done, B)
                pick(g, T // 2)
            power(2, rstd, veps, var_ready, rstd_ready)
            power(3, rstd, veps, var_ready, rstd_ready)

        @block.scalar
        def _(act):
            def dst_rep_load(c):
                i0 = c * CT
                for p0, t0, n in RUNS:
                    a, z = max(i0, p0), min(i0 + CT, p0 + n)
                    if a < z:
                        t = t0 + a - p0
                        act.dma_start(dst_rep[:, c % 4, (a - i0) * P:(z - i0) * P],
                                      dst[t * P:(t + z - a) * P].partition_broadcast(P)).then_inc(dst_in[c % 4], 16)

            for b in range(B):
                act.wait_ge(h_pre, b + 1)
                act.activation(xf[:, b, :], xf[:, b, :], ACT.Relu).then_inc(h_ready, 1)
            for c in range(4):
                dst_rep_load(c)
            for f in range(K):
                act.wait_ge(hT_ready, f + 1)
                act.activation(fT_hi[:, f, :], bank[f][:, :], ACT.Copy).then_inc(fT_hi_done, 1)

            def hi_quad(c0, lap, pe_free):
                for r in range(4):
                    act.wait_ge(w_in[r % 2], lap * 32 + 16 * (r // 2 + 1))
                    if pe_free:
                        act.wait_ge(chunk_used, c0 + (r - 3))
                    act.activation(w_hi[:, r, :], w_raw[:, r % 2, :], ACT.Copy).then_inc(hi_done, 1)

            def evacuate(u):
                for j in range(8):
                    e = 8 * u + j
                    bank_ready(act, u, j)
                    if e >= 4:
                        act.wait_ge(stored[e % 4], 16 * (e // 4))
                    act.activation(stage[:, e % 4, :], bank[j][:, :], ACT.Copy).then_inc(evac, 1)

            def replicate_lift(c):
                act.wait_ge(lift_ready, c + 1)
                for a in range(0, P, 32):
                    act.dma_start(lift_row[c, :, a:a + 32], liftT[a:a + CT, c % 2, :]).then_inc(lift_out, 16)
                act.wait_ge(lift_out, 16 * 4 * (c + 1))
                if c >= 1:
                    act.wait_ge(max_done, 2 * B * c)
                act.dma_start(lift[:, :], lift_row[c].rearrange("t p -> (t p)").partition_broadcast(P)).then_inc(lift_in, 16)

            hi_quad(0, 0, False)
            for c in range(4, NC):
                act.wait_ge(member_done, c - 3)
                dst_rep_load(c)
            for u in range(UNITS):
                with act.Fori(2 * u + 1, 2 * u + 3) as q:
                    hi_quad(q * 4, q, True)
                if u % 2 == 0:
                    evacuate(u)
                if u >= 3:
                    replicate_lift(u - 3)
            with act.Fori(2 * UNITS + 1, 2 * UNITS + 3) as q:
                hi_quad(q * 4, q, True)
            replicate_lift(3)
            with act.Fori(2 * UNITS + 3, 2 * UNITS + 5) as q:
                hi_quad(q * 4, q, True)
            for c in range(4, NC):
                replicate_lift(c)
            act.wait_ge(arg_ready, 1)
            act.activation(ex[:, :], me[:, :], ACT.Exp, scale=-1.0).then_inc(ex_ready, 1)
            act.wait_ge(h_back, 16)
            for b in range(B):
                act.activation(hn_hi[:, b, :], hf[:, b, :], ACT.Copy).then_inc(hn_hi_done, 1)
            for s in range(B):
                act.wait_ge(adjT_done, B + s + 1)
                act.activation(adjT_hi[:, s, :], bank[4 + s][:, :], ACT.Copy).then_inc(adjT_hi_done, 1)
            for f in range(K):
                act.wait_ge(z_done, f + 1)
                act.activation(fT_hi[:, f, :], bank[f][:, :], ACT.Copy).then_inc(fT_hi_done, 1)
            for s in range(B):
                act.activation(adjT_hi[:, s, :], adjwT[:, s, :], ACT.Copy).then_inc(adjT_hi_done, 1)
            with act.Fori(C_BOT // 4 + 1, C_L1 // 4) as q:
                hi_quad(q * 4, q, True)
            hi_quad(C_L1, C_L1 // 4, True)
            for n, b in enumerate((1, 2, 3, 0)):
                act.wait_ge(h_pre, B + n + 1)
                act.activation(hn_hi[:, b, :], hf[:, b, :], ACT.Relu).then_inc(hn_hi_done, 1)
            for f in range(K):
                act.wait_ge(z_done, K + f + 1)
                act.activation(fT_hi[:, f, :], bank[f][:, :], ACT.Copy).then_inc(fT_hi_done, 1)
            hi_quad(C_L1 + 4, C_L1 // 4 + 1, True)

        @block.vector
        def _(dve):
            step = Step(dve, own)

            def build_member(c):
                dve.wait_ge(dst_in[c % 4], 16 * dst_loads(c))
                for b in range(B):
                    ins = dve.tensor_scalar(member[:, b, c * CE:(c + 1) * CE], dst_rep[:, c % 4, :],
                                            node_id[:, b:b + 1], 0.0, ALU.is_equal, ALU.add,
                                            accum_out=count[:, b, c:c + 1])
                ins.then_inc(member_done, 1)

            def dst_loads(c):
                total = 0
                for cc in range(c % 4, c + 1, 4):
                    for p0, t0, n in RUNS:
                        total += max(cc * CT, p0) < min(cc * CT + CT, p0 + n)
                return total

            def norm_stats(blocks, arrived=None):
                for b in blocks:
                    if arrived is not None:
                        dve.wait_ge(arrived[b], 16)
                    for n in range(2):
                        ins = dve.bn_stats(stats[:, b, n, :], xf[:, b, n * H:(n + 1) * H])
                    step(ins)
                    ins = dve.bn_aggr(mv[:, b, :], stats[:, b, :, :])
                    step(ins)

            norm_stats(range(B), x_in)
            dve.tensor_scalar(veps[:, :], mv[:, :, 1], EPS, None, ALU.add).then_inc(var_ready, 1)
            dve.wait_ge(rstd_ready, 1)
            for b in range(B):
                dve.tensor_scalar(xf[:, b, :], xf[:, b, :], mv[:, b, 0:1], rstd[:, b:b + 1], ALU.subtract,
                                  ALU.mult).then_inc(h_pre, 1)
            dve.wait_ge(ids_in, 16 * 3 * len(RUNS))
            step(dve.tensor_copy(ids_rowf[:, 0:2, :], ids_row[:, 0:2, :]))
            dve.wait_ge(consts, 7)
            block_no = ids_row[:, 0, :].bitcast(F32)
            step(dve.tensor_scalar(block_no, ids_rowf[:, 1, :], float(P), None, ALU.is_ge))
            for b in range(2, B):
                step(dve.scalar_tensor_tensor(block_no, ids_rowf[:, 1, :], float(b * P), block_no, ALU.is_ge, ALU.add))
            dve.tensor_reduce(tile_lo[:, 0:1], block_no, AX.X, ALU.min)
            dve.tensor_reduce(tile_lo[:, 1:2], block_no, AX.X, ALU.max).then_inc(idsf_ready, 1)
            dve.wait_ge(idsT_ready, 1)
            step(dve.tensor_copy(ids_f[:, :, :], bank[0][:, 0:3 * T].rearrange("p (a t) -> p a t", a=3)))
            dve.tensor_copy(ids_i[:, :, :], ids_f[:, 0:2, :]).then_inc(ids_ready, 1)
            for k, op in enumerate((ALU.min, ALU.max)):
                step(dve.tensor_reduce(pair_row[:, k, :], bank[0][0:1, (3 + k) * T:(4 + k) * T].rearrange(
                    "o (p r) -> o p r", r=2), AX.X, op))
            for k in range(4):
                ins = dve.memset(nibble[:, :, k:k + 1], float(16 ** k))
            step(ins)
            step(dve.scalar_tensor_tensor(pair_row[:, 2, :], pair_row[:, 1, :], 4.0, pair_row[:, 0, :], ALU.mult, ALU.add))
            step(dve.tensor_tensor(nibble[:, :, :], nibble[:, :, :], pair_row[:, 2, :].rearrange("o (w k) -> o w k", k=4),
                                   ALU.mult))
            step(dve.tensor_reduce(pair_row[:, 0, 0:T // 8], nibble[:, :, :], AX.X, ALU.add))
            dve.tensor_copy(pair_word[:, :], pair_row[:, 0, 0:T // 8]).then_inc(words_ready, 1)

            def split3(parts, whole, n):
                src_ap = whole
                for k in range(3):
                    step(dve.tensor_copy(part16[:, :], src_ap))
                    step(dve.tensor_copy(parts[:, k, :], part16[:, :]))
                    if k < 2:
                        step(dve.tensor_tensor(rest[:, :], src_ap, parts[:, k, :], ALU.subtract))
                        src_ap = rest[:, :]

            for f in range(K):
                dve.wait_ge(fT_hi_done, f + 1)
                dve.tensor_tensor(fT_lo[:, f, :], bank[f][:, :], fT_hi[:, f, :].bitcast(F32), ALU.subtract
                                  ).then_inc(fT_lo_done, 1)

            def lo(c0, r, pe_free):
                dve.wait_ge(hi_done, c0 + (r + 1))
                if pe_free:
                    dve.wait_ge(chunk_used, c0 + (r - 3))
                dve.tensor_tensor(w_lo[:, r, :], w_raw[:, r % 2, :], w_hi[:, r, :].bitcast(F32), ALU.subtract
                                  ).then_inc(lo_done, 1)

            def edge(i, r, lap):
                dve.wait_ge(row_in[r], lap * 32 + 32)
                dve.scalar_tensor_tensor(rows[:, r, :], rows[:, r, :], 0.0, wa_rep[:, :], ALU.max, ALU.mult,
                                         accum_out=logit[:, bass.ds(i, 1)]).then_inc(edge_done, 1)

            def lift_chunk(c):
                a, z = c * CT, (c + 1) * CT
                dve.wait_ge(edge_done, z)
                step(dve.tensor_scalar(lb[:, a:z], logit[:, a:z], ba_rep[:, 0:1], None, ALU.add))
                step(dve.tensor_scalar(lifted[:, c % 2, 0:CT], lb[:, a:z], BIG, None, ALU.add))
                if c >= 2:
                    dve.wait_ge(lift_out, 16 * 4 * (c - 1))
                dve.transpose(liftT[:, c % 2, :], lifted[:, c % 2, :]).then_inc(lift_ready, 1)

            def chunk_max(c):
                dve.wait_ge(lift_in, 16 * (c + 1))
                for n in range(2 * B):
                    b, h = n // 2, n % 2
                    a, z = h * CE // 2, (h + 1) * CE // 2
                    if c or n:
                        dve.wait_ge(max_done, 2 * B * c + n)
                    dve.tensor_tensor_reduce(masked[:, :], lift[:, a:z], member[:, b, c * CE + a:c * CE + z], 1.0, 0.0,
                                             ALU.mult, ALU.max, cmax[:, b, 2 * c + h:2 * c + h + 1]).then_inc(max_done, 1)

            def evacuate(u):
                kind = u // 2
                dve.wait_ge(bias_in[kind % 2], 16 * (kind // 2 + 1))
                for j in range(8):
                    e = 8 * u + j
                    bank_ready(dve, u, j)
                    dve.wait_ge(stored[e % 4], 16 * (e // 4))
                    n = j % 2
                    dve.tensor_tensor(stage[:, e % 4, :], bank[j][:, :], bias[:, kind % 2, n * H:(n + 1) * H],
                                      ALU.add).then_inc(evac, 1)

            for r in range(4):
                lo(0, r, False)
            split3(w_part, ids_f[:, 2, :], T)
            step(dve.memset(lifted[:, :, :], 0.0))
            for c in range(4):
                build_member(c)
            dve.wait_ge(wa_in, 32)
            for u in range(UNITS + 1):
                with dve.Fori(2 * u + 1, 2 * u + 3) as q:
                    for r in range(4):
                        lo(q * 4, r, True)
                        if u >= 2:
                            edge(q * 4 + (r - 8 * u - 4 + 8 * (u - 2)), r, q - (2 * u + 1) + 2 * (u - 2))
                if u < UNITS and u % 2 == 1:
                    evacuate(u)
                if u == 0:
                    for c in range(4, NC):
                        build_member(c)
                    dve.wait_ge(member_done, NC)
                    step(dve.tensor_reduce(deg_in[:, :], count[:, :, :], AX.X, ALU.add))
                if u >= 2:
                    lift_chunk(u - 2)
                if u >= 4:
                    chunk_max(u - 4)
            with dve.Fori(2 * UNITS + 3, 2 * UNITS + 4) as q:
                for r in range(4):
                    lo(q * 4, r, True)
            dve.wait_ge(bias_in[1], 32)
            dve.wait_ge(bias_in[0], 48)
            dve.wait_ge(h_out, 16)
            for j in (2, 3, 4, 5, 6, 7, 0, 1):
                m, n = j // 2, j % 2
                bank_ready(dve, UNITS, j)
                dve.tensor_tensor(xf[:, m, n * H:(n + 1) * H], bank[j][:, :],
                                  bias[:, 0 if m < BLOCK_H else 1, n * H:(n + 1) * H], ALU.add).then_inc(evac, 1)
            with dve.Fori(2 * UNITS + 4, 2 * UNITS + 5) as q:
                for r in range(4):
                    lo(q * 4, r, True)

            def spread(t, slot, r, parts):
                for k in range(3):
                    ins = dve.tensor_scalar(pick_dst[slot][:, r, k, :], node_no[:, :], ids_f[:, 1, bass.ds(t, 1)],
                                            parts[:, k, bass.ds(t, 1)], ALU.is_equal, ALU.mult)
                ins.then_inc(dst_ready, 1)

            MIX = 40
            for q in range((T - MIX) // 4):
                for i in range(4):
                    t = MIX + 4 * q + i
                    edge(t, t % 4, t // 4)
                    for g in range(8 * q + 2 * i, 8 * q + 2 * i + 2):
                        if g == 2:
                            for s in range(4):
                                dve.wait_ge(stored[s], 2 * 16 * UNITS)
                        if g >= 4 and g % 2 == 0:
                            dve.wait_ge(adj_done, g // 2 - 1)
                        spread(g, g // 2 % 2, g % 2, w_part)
                if q % 2 == 1:
                    lift_chunk(MIX // 8 + q // 2)
                if q in (0, 2, 4):
                    chunk_max(UNITS - 3 + q // 2)
            chunk_max(6)
            with dve.Fori((T - 16) // 4, T // 4) as q:
                for r in range(4):
                    if r % 2 == 0:
                        dve.wait_ge(adj_done, q * 2 + (r // 2 - 1))
                    spread(q * 4 + r, r // 2, r % 2, w_part)
            chunk_max(7)
            dve.wait_ge(max_done, 2 * B * NC)
            step(dve.tensor_reduce(mx[:, :], cmax[:, :, :], AX.X, ALU.max))
            left = mx
            for k in range(3):
                ins = dve.tensor_copy(mpart[:, :, k], left[:, :])
                if k == 2:
                    ins.then_inc(mpart_ready, 1)
                else:
                    step(ins)
                    step(dve.tensor_tensor(mrest[:, :], left[:, :], mpart[:, :, k], ALU.subtract))
                    left = mrest
            dve.wait_ge(me_done, 1)
            step(dve.tensor_reduce(me[:, :], bank[5][:, 0:3 * T].rearrange("p (t k) -> p t k", k=3), AX.X, ALU.add))
            step(dve.tensor_scalar(rest[:, :], me[:, :], -BIG, None, ALU.add))
            dve.tensor_tensor(me[:, :], rest[:, :], lb[:, :], ALU.subtract).then_inc(arg_ready, 1)
            dve.wait_ge(adj_full, 1)
            for b in range(B):
                ins = dve.tensor_reduce(wsum[:, b:b + 1], bank[b][:, :], AX.X, ALU.add)
                dve.tensor_copy(adj[:, b, :], bank[b][:, :]).then_inc(adj_ready, 1)
            step(ins)
            step(dve.tensor_scalar(wsum[:, :], wsum[:, :], TINY, None, ALU.max))
            step(dve.tensor_scalar(deg_in[:, :], deg_in[:, :], 1.0, None, ALU.max))
            step(dve.tensor_tensor(mrest[:, :], wsum[:, :], deg_in[:, :], ALU.mult))
            dve.tensor_copy(wsum[:, :], mrest[:, :]).then_inc(wsum_ready, 1)
            step(dve.tensor_scalar(deg_out[:, :], bank[4][:, 0:B], 1.0, None, ALU.max))
            dve.wait_ge(wout_done, 1)
            step(dve.tensor_scalar(mrest[:, :], bank[6][:, 0:B], TINY, None, ALU.max))
            dve.tensor_tensor(w_out[:, :], mrest[:, :], deg_out[:, :], ALU.mult).then_inc(wdeg_ready, 1)
            dve.wait_ge(ex_ready, 1)
            split3(e_part, ex[:, :], T)
            dve.wait_ge(fac_ready, 2)
            for b in range(B):
                dve.tensor_scalar(adj[:, b, :], adj[:, b, :], f_dst[:, b:b + 1], None, ALU.mult).then_inc(adj_ready, 1)
            for s in range(B):
                dve.wait_ge(adjT_done, s + 1)
                dve.tensor_copy(adjwT[:, s, :], bank[4 + s][:, :]).then_inc(adjwT_ready, 1)
            with dve.Fori(0, T // 4) as q:
                for r in range(4):
                    if r % 2 == 0:
                        dve.wait_ge(adj_done, q * 2 + (T // 2 + r // 2 - 1))
                    spread(q * 4 + r, r // 2, r % 2, e_part)
            for b in range(B):
                dve.wait_ge(hn_hi_done, b + 1)
                dve.tensor_tensor(hn_lo[:, b, :], hf[:, b, :], hn_hi[:, b, :].bitcast(F32), ALU.subtract
                                  ).then_inc(hn_lo_done, 1)
            dve.wait_ge(adj_full, 2)
            for b in range(B):
                ins = dve.tensor_reduce(wsum[:, b:b + 1], bank[b][:, :], AX.X, ALU.add)
            step(ins)
            step(dve.tensor_scalar(wsum[:, :], wsum[:, :], TINY, None, ALU.max))
            step(dve.reciprocal(rden[:, :], wsum[:, :]))
            for b in range(B):
                dve.tensor_scalar(adj[:, b, :], bank[b][:, :], rden[:, b:b + 1], None, ALU.mult).then_inc(adj_ready, 1)

            def low_of(dst_t, s, psum, hi_t, hi_sem, hi_n, done):
                dve.wait_ge(hi_sem, hi_n)
                dve.tensor_tensor(dst_t[:, s, :], psum, hi_t[:, s, :].bitcast(F32), ALU.subtract).then_inc(done, 1)

            for s in range(B):
                low_of(adjT_lo, s, bank[4 + s][:, :], adjT_hi, adjT_hi_done, s + 1, adjT_lo_done)
            for f in range(K):
                low_of(fT_lo, f, bank[f][:, :], fT_hi, fT_hi_done, K + f + 1, fT_lo_done)
            for s in range(B):
                low_of(adjT_lo, s, adjwT[:, s, :], adjT_hi, adjT_hi_done, B + s + 1, adjT_lo_done)
            with dve.Fori(C_BOT // 4 + 1, C_L1 // 4) as q:
                for r in range(4):
                    lo(q * 4, r, True)
            for r in range(4):
                lo(C_L1, r, True)
            dve.wait_ge(x_again, 16 * B)
            for g, blocks in enumerate(((1, 2, 3), (0,))):
                for m in blocks:
                    for n in range(2):
                        j, a, z = 2 * m + n, n * H, (n + 1) * H
                        bank_ready(dve, UNITS + 1, j)
                        step(dve.tensor_tensor(xf[:, m, a:z], bank[j][:, :], xf[:, m, a:z], ALU.add))
                        ins = dve.scalar_tensor_tensor(xf[:, m, a:z], xf[:, m, a:z], 0.0, hf[:, m, a:z], ALU.max,
                                                       ALU.add)
                        ins.then_inc(x2_step, 1)
                    dve.wait_ge(x2_step, 2 * ((m - 1) % B) + 2)
                norm_stats(blocks)
                b0, b1 = blocks[0], blocks[-1] + 1
                if g == 0:
                    step(dve.memset(mv[:, 0, 1:2], 1.0))
                dve.tensor_scalar(veps[:, :], mv[:, :, 1], EPS, None, ALU.add).then_inc(var_ready, 1)
                dve.wait_ge(rstd_ready, 2 + g)
                step(dve.tensor_tensor(rstd[:, b0:b1], rstd[:, b0:b1], f_src[:, b0:b1], ALU.mult))
                for m in blocks:
                    dve.tensor_scalar(hf[:, m, :], xf[:, m, :], mv[:, m, 0:1], rstd[:, m:m + 1], ALU.subtract,
                                      ALU.mult).then_inc(h_pre, 1)
                for m in blocks:
                    n = (m - 1) % B
                    dve.wait_ge(hn_hi_done, B + n + 1)
                    dve.scalar_tensor_tensor(hn_lo[:, m, :], hf[:, m, :], 0.0, hn_hi[:, m, :].bitcast(F32), ALU.max,
                                             ALU.subtract).then_inc(hn_lo_done, 1)
            for f in range(K):
                low_of(fT_lo, f, bank[f][:, :], fT_hi, fT_hi_done, 2 * K + f + 1, fT_lo_done)
            for r in range(4):
                lo(C_L1 + 4, r, True)
            dve.wait_ge(bias_in[1], 48)
            for j in range(8):
                m, n = j // 2, j % 2
                a, z = n * H, (n + 1) * H
                bank_ready(dve, UNITS + 2, j)
                if j >= 4:
                    dve.wait_ge(out_stored[j % 4], 16)
                step(dve.tensor_tensor(stage[:, j % 4, :], bank[j][:, :], bias[:, 1, a:z], ALU.add))
                dve.scalar_tensor_tensor(stage[:, j % 4, :], stage[:, j % 4, :], 0.0, xf[:, m, a:z], ALU.max,
                                         ALU.add).then_inc(out_ready, 1)

        @block.tensor
        def _(pe):
            pe.wait_ge(consts, 7)
            pe.wait_ge(idsf_ready, 1)
            for a in range(3):
                ins = pe.transpose(bank[0][:, a * T:(a + 1) * T], ids_rowf[:, a, :], ident[0:T, 0:T])
            for k in range(2):
                ins = pe.transpose(bank[0][0:1, (3 + k) * T:(4 + k) * T], tile_lo[:, k:k + 1], ident[0:T, 0:T])
            ins.then_inc(idsT_ready, 1)
            pe.wait_ge(h_ready, B)
            pe.wait_ge(words_ready, 1)
            pe.wait_ge(ids_ready, 1)
            for f in range(K):
                for b in range(B):
                    ins = pe.transpose(bank[f][:, b * P:(b + 1) * P], xf[:, b, f * P:(f + 1) * P], ident[:, :])
                ins.then_inc(hT_ready, 1)

            def chunk(c, k, slot, banks, evac_wait):
                pe.wait_ge(lo_done, c + 1)
                for j in banks:
                    if k == 0 and evac_wait is not None:
                        pe.wait_ge(evac, evac_wait + (j + 1))
                    m, n = j // 2, j % 2
                    for p, (a, b) in enumerate(AB):
                        ins = pe.matmul(bank[j][:, :], fT[a][:, k, m * P:(m + 1) * P],
                                        wS[b][:, slot, n * H:(n + 1) * H],
                                        start=(k == 0 and p == 0), stop=(k == K - 1 and p == 2))
                    if k == K - 1 and j != banks[-1]:
                        ins.then_inc(bank_done, 1)
                ins.then_inc(chunk_used, 1)

            ALL = range(8)
            pe.wait_ge(fT_lo_done, K)
            for k in range(K):
                chunk(k, k, k % 4, ALL, None)
            with pe.Fori(1, UNITS) as u:
                for k in range(K):
                    chunk(u * K + k, k, k % 4, ALL, u * 8 - 8)
            for k in range(K):
                chunk(C_TOP + k, k, k % 4, range(2, 8), 8 * UNITS - 8)
            for k in range(K):
                chunk(C_TOP + K + k, k, k % 4, range(2), 8 * UNITS - 8)

            def adj_clear():
                for b in range(B):
                    pe.matmul(bank[b][:, :], zeros[:, :], node_no[:, :], start=True, stop=True)
                pe.matmul(bank[4][:, 0:B], zeros[:, :], node_no[:, 0:B], start=True, stop=True)

            def adj_close(deg):
                if deg:
                    pe.matmul(bank[4][:, 0:B], zeros[:, :], node_no[:, 0:B], start=False, stop=True,
                              skip_group_check=True)
                for b in range(B):
                    ins = pe.matmul(bank[b][:, :], zeros[:, :], node_no[:, :], start=False, stop=True,
                                    skip_group_check=True)
                ins.then_inc(adj_full, 1)

            def adj_sum(first_pair, deg):
                with pe.Fori(0, T // 8) as q:
                    word = pe.value_load(pair_word[0:1, bass.ds(q, 1)], min_val=0, max_val=16 ** 4 - 1)
                    for k in range(4):
                        slot = k % 2
                        lo, hi = pe.snap((word >> (4 * k)) & 3), pe.snap((word >> (4 * k + 2)) & 3)
                        pe.wait_ge(src_ready, q * 8 + (2 * first_pair + 2 * k + 2))
                        pe.wait_ge(dst_ready, q * 8 + (2 * first_pair + 2 * k + 2))
                        if deg:
                            for r in range(2):
                                for b in range(B):
                                    pe.matmul(bank[4][:, b:b + 1], pick_src[slot][:, r, b * P:(b + 1) * P],
                                              ones_b[:, :], start=False, stop=True, skip_group_check=True)
                        with pe.Fori(lo, hi + 1) as b:
                            for r in range(2):
                                for p in range(3):
                                    pe.matmul(banks[:, bass.ds(b * H, H)], pick_dst[slot][:, r, p, bass.ds(b * P, P)],
                                              pick_src[slot][:, r, :], start=False, stop=True, skip_group_check=True)
                        pe.matmul(bank[4][:, 0:B], zeros[:, :], node_no[:, 0:B], start=False, stop=True,
                                  skip_group_check=True).then_inc(adj_done, 1)

            def transpose_adj(n):
                for b in range(B):
                    pe.wait_ge(adj_ready, n + b + 1)
                for s in range(B):
                    for b in range(B):
                        ins = pe.transpose(bank[4 + s][:, b * P:(b + 1) * P], adj[:, b, s * P:(s + 1) * P], ident[:, :])
                    ins.then_inc(adjT_done, 1)

            pe.wait_ge(evac, 8 * UNITS + 8)
            adj_clear()
            adj_sum(0, True)
            adj_close(True)
            pe.wait_ge(mpart_ready, 1)
            with pe.Fori(0, T // 4) as q:
                for r in range(4):
                    for b in range(B):
                        ins = pe.matmul(bank[5][:, bass.ds(q * 12 + 3 * r, 3)],
                                        member[:, b, bass.ds(q * (4 * P) + r * P, P)], mpart[:, b, :],
                                        start=(b == 0), stop=(b == B - 1))
            for b in range(B):
                ins = pe.matmul(bank[5][:, 3 * T - 3:3 * T], member[:, b, E - P:E], mpart[:, b, :],
                                start=(b == 0), stop=(b == B - 1))
            ins.then_inc(me_done, 1)
            pe.wait_ge(adj_ready, B)
            for s in range(B):
                for b in range(B):
                    ins = pe.matmul(bank[6][:, s:s + 1], adj[:, b, s * P:(s + 1) * P], ones_f[:, :],
                                    start=(b == 0), stop=(b == B - 1))
            ins.then_inc(wout_done, 1)
            pe.wait_ge(arg_ready, 1)
            pe.wait_ge(wdeg_ready, 1)
            transpose_adj(B)
            pe.wait_ge(adjwT_ready, B)
            adj_clear()
            adj_sum(T // 2, False)
            adj_close(False)
            transpose_adj(2 * B)

            def features(order, n_adj, n_hn, n_free, free_sem):
                for i, s in enumerate(order):
                    pe.wait_ge(adjT_lo_done, n_adj + (s + 1 if i == 0 or n_adj == 0 else B))
                    pe.wait_ge(hn_lo_done, n_hn + i + 1)
                    for f in range(K):
                        if i == 0 and free_sem is not None and f >= 4:
                            pe.wait_ge(adjT_lo_done, f - 3)
                        for p, (a, b) in enumerate(AB):
                            ins = pe.matmul(bank[f][:, :], hn[a][:, s, f * P:(f + 1) * P], adjT[b][:, s, :],
                                            start=(i == 0 and p == 0), stop=(i == B - 1 and p == 2))
                        if i == B - 1:
                            ins.then_inc(z_done, 1)

            features((0, 1, 2, 3), 0, 0, 0, True)
            pe.wait_ge(fT_lo_done, 2 * K)
            for k in range(K):
                chunk(C_BOT + k, k, k % 4, range(2, 8), None)
            for k in range(K):
                chunk(C_BOT + K + k, k, k % 4, range(2), None)
            pe.wait_ge(x2_step, 8)
            pe.wait_ge(adjT_lo_done, 2 * B)
            features((1, 2, 3, 0), B, B, 0, None)
            pe.wait_ge(fT_lo_done, 3 * K)
            for k in range(K):
                chunk(C_L1 + k, k, k % 4, ALL, None)


_INS = ["x", "src", "dst", "edge_weight", "L0_gnn_W_hh", "L0_gnn_b_hh", "L0_gnn_W_oo", "L0_gnn_b_oo", "L0_gnn_W_ho",
        "L0_gnn_b_ho", "L0_gnn_W_a", "L0_gnn_b_a", "L0_gnn_W_hn", "L0_gnn_b_hn", "L0_gnn_W_on", "L0_gnn_b_on",
        "L1_gnn_W", "L1_gnn_b"]


def kernel(**inputs):
    import numpy as _np
    import concourse.bacc as _bacc
    from concourse import mybir as _mybir
    from concourse.bass_utils import run_bass_kernel_spmd as _run

    nc = _bacc.Bacc("TRN2", target_bir_lowering=False, num_devices=1)
    arrays, args = {}, []
    for name in _INS:
        a = _np.ascontiguousarray(inputs[name])
        arrays[f"in_{name}_dram"] = a
        args.append(nc.dram_tensor(f"in_{name}_dram", a.shape, _mybir.dt.from_np(a.dtype), kind="ExternalInput").ap())
    out = nc.dram_tensor("out_0_dram", inputs["x"].shape, _mybir.dt.float32, kind="ExternalOutput").ap()
    build(nc, *args, out)
    r = _run(nc, [arrays], core_ids=[0])
    return r.results[0]["out_0_dram"]
```

```python
from contextlib import ExitStack

import concourse.bass as bass
from concourse import mybir
from concourse.alu_op_type import AluOpType as ALU

ACT = mybir.ActivationFunctionType
AX = mybir.AxisListType
F32, F32R, BF16, F16 = mybir.dt.float32, mybir.dt.float32r, mybir.dt.bfloat16, mybir.dt.float16
F8, I32 = mybir.dt.float8e4, mybir.dt.int32

P = 128
EPS = 1e-5
TINY = 1e-30
BIG = float(2 ** 20)

TILE_HH, TILE_OO = 2, 12
BLOCK_H = 1


def tile_order(T):
    first = 16
    runs = [(0, first, T - first)]
    runs.append((T - first, TILE_OO, first - TILE_OO))
    runs.append((T - TILE_OO, TILE_HH, TILE_OO - TILE_HH))
    runs.append((T - TILE_HH, 0, TILE_HH))
    return runs


class Step:

    def __init__(self, eng, sem):
        self.eng, self.sem, self.n = eng, sem, 0

    def __call__(self, ins):
        self.n += 1
        ins.then_inc(self.sem, 1)
        self.eng.wait_ge(self.sem, self.n)


def build(nc, x, src, dst, edge_w, W_hh, b_hh, W_oo, b_oo, W_ho, b_ho, W_a, b_a, W_hn, b_hn, W_on, b_on,
          W_1, b_1, out):
    N, D = x.shape
    E = src.shape[0]
    B, K, T = N // P, D // P, E // P
    H = D // 2
    CT = 8
    NC = T // CT
    CE = CT * P
    RUNS = tile_order(T)
    TE = T - TILE_HH
    kind_of = lambda i: 0 if i < T - TILE_OO else 1

    kinds = [(W_ho, b_ho), (W_oo, b_oo)]
    UNITS = 2 * len(kinds)
    C_TOP = K * UNITS
    C_HH = C_TOP + 2 * K
    C_BOT = C_HH + 2 * K
    C_L1 = C_BOT + 2 * K
    C_END = C_L1 + K

    def chunk_rows(c):
        if c < C_TOP:
            u, k = c // K, c % K
            w, row = kinds[u // 2][0], (u % 2) * D + k * P
        elif C_HH <= c < C_BOT:
            w, row = W_hh, (c - C_HH) * P
        elif c < C_L1:
            bottom = c >= C_BOT
            q, k = (c - (C_BOT if bottom else C_TOP)) // K, c % K
            w, row = (W_hn if bool(q) != bottom else W_on), bottom * D + k * P
        else:
            w, row = W_1, (c - C_L1) * P
        return w[row:row + P, :]

    with ExitStack() as ctx:
        place = [(nc.sbuf_base + 31) // 32 * 32]
        size = {F32: 4, F32R: 4, I32: 4, BF16: 2, F16: 2, F8: 1}

        def sb(name, shape, dt, over=None):
            n = size[dt]
            for d in shape[1:]:
                n *= d
            at = place[0] if over is None else over
            t = nc.alloc_sbuf_tensor_at(name, shape, dt, offset=at)
            if over is None:
                place[0] += (n + 31) // 32 * 32
                assert place[0] <= nc.sbuf_usable_end, (name, place[0])
            return t, at

        def sem(name):
            return ctx.enter_context(nc.semaphore(name))

        banks = ctx.enter_context(nc.psum_tensor("banks", [P, 8 * H], F32))
        bank = [banks[:, i * H:(i + 1) * H] for i in range(8)]

        xf, _ = sb("xf", [P, B, D], F32)
        fT_hi, _ = sb("fT_hi", [P, K, N], F32R)
        fT_lo, _ = sb("fT_lo", [P, K, N], F32R)
        w_raw, _ = sb("w_raw", [P, 2, D], F32)
        w_hi, at = sb("w_hi", [P, 4, D], F32R)
        w_lo, _ = sb("w_lo", [P, 4, D], F32R)
        RING = 4
        pair_size = 2 * (3 + 1) * N * 2
        pick_dst = [sb(f"pick_dst{r}", [P, 2, 3, N], BF16, over=at + r * pair_size)[0] for r in range(RING)]
        pick_src = [sb(f"pick_src{r}", [P, 2, N], BF16, over=at + r * pair_size + 2 * 3 * N * 2)[0]
                    for r in range(RING)]
        member, at = sb("member", [P, B, E], BF16)
        hn_hi, _ = sb("hn_hi", [P, B, D], F32R, over=at)
        hn_lo, _ = sb("hn_lo", [P, B, D], F32R, over=at + B * D * 4)
        hf, _ = sb("hf", [P, B, D], F32, over=at + 2 * B * D * 4)
        adjwT, _ = sb("adjwT", [P, B, N], F32, over=at + 3 * B * D * 4)
        ROWS = 6
        rows, at = sb("rows", [P, ROWS, D], F32)
        dst_rep, _ = sb("dst_rep", [P, 4, CE], I32, over=at)
        adjT_hi, _ = sb("adjT_hi", [P, B, N], F32R, over=at)
        adjT_lo, _ = sb("adjT_lo", [P, B, N], F32R, over=at + B * N * 4)
        stage, at = sb("stage", [P, 4, H], F32)
        h_edge, _ = sb("h_edge", [P, TILE_HH, D], F32, over=at)
        adj, _ = sb("adj", [P, B, N], F32, over=at)
        wa_rep, _ = sb("wa_rep", [P, D], F32)
        bias, _ = sb("bias", [P, 2, D], F32)
        lift, at = sb("lift", [P, CE], F32)
        ids_row, _ = sb("ids_row", [T, 2, P], I32, over=at)
        ids_rowf, _ = sb("ids_rowf", [T, 3, P], F32, over=at + 2 * P * 4)
        masked, at = sb("masked", [P, CE // 2], BF16)
        e_part, _ = sb("e_part", [P, 3, T], F32, over=at)
        pair_row, _ = sb("pair_row", [1, 3, T // 2], F32, over=at)
        nibble, _ = sb("nibble", [1, T // 8, 4], F32, over=at + 3 * T // 2 * 4)
        ident, _ = sb("ident", [P, P], F32)
        node_no, _ = sb("node_no", [P, N], F16)
        zeros, _ = sb("zeros", [P, P], BF16)
        ids_f, _ = sb("ids_f", [P, 3, T], F32)
        ids_i, _ = sb("ids_i", [P, 2, T], I32)
        node_id, _ = sb("node_id", [P, B], F32)
        w_part, _ = sb("w_part", [P, 3, T], F32)
        pair_end, _ = sb("pair_end", [P, T // 2], BF16)
        tile_lo, _ = sb("tile_lo", [T, 2], F32)
        pair_word, _ = sb("pair_word", [1, T // 8], I32)
        w_col, at = sb("w_col", [P, T, 4], BF16)
        part16, _ = sb("part16", [P, T], BF16)
        rest, _ = sb("rest", [P, T], F32, over=at)
        at_w = at
        logit, at = sb("logit", [P, T], F32)
        ex, _ = sb("ex", [P, T], F32, over=at)
        lb, _ = sb("lb", [P, T], F32)
        lifted, _ = sb("lifted", [P, 2, 32], F32)
        liftT, _ = sb("liftT", [P, 2, 32], F32)
        me, _ = sb("me", [P, T], F32, over=at_w + T * 4)
        ba_rep, _ = sb("ba_rep", [P, 1], F32)
        ones_f, _ = sb("ones_f", [P, 1], F32)
        nhalf, _ = sb("nhalf", [P, B], F32)
        stats, _ = sb("stats", [P, B, 2, 6], F32)
        mv, _ = sb("mv", [P, B, 2], F32)
        veps, _ = sb("veps", [P, B], F32)
        rstd, _ = sb("rstd", [P, B], F32)
        count, _ = sb("count", [P, B, NC], F32)
        cmax, _ = sb("cmax", [P, B, 2 * NC], F32)
        deg_in, _ = sb("deg_in", [P, B], F32)
        deg_out, _ = sb("deg_out", [P, B], F32)
        wsum, _ = sb("wsum", [P, B], F32)
        w_out, _ = sb("w_out", [P, B], F32)
        f_dst, _ = sb("f_dst", [P, B], F32)
        f_src, _ = sb("f_src", [P, B], F32)
        rden, _ = sb("rden", [P, B], F32)
        mx, _ = sb("mx", [P, B], F32)
        mrest, _ = sb("mrest", [P, B], F32)
        mpart, _ = sb("mpart", [P, B, 3], BF16)

        table = [[nc.dram_tensor(f"table{k}{s}", [N, D], F32, kind="Internal").ap() for s in range(2)]
                 for k in range(3)]
        h_row = nc.dram_tensor("h_row", [N, D], F32, kind="Internal").ap()
        lift_row = nc.dram_tensor("lift_row", [NC, CT, P], F32, kind="Internal").ap()

        h_out = sem("h_out"); hh_in = [sem(f"hh_in{r}") for r in range(TILE_HH)]; hhT_ready = sem("hhT_ready"); hh_hi_done = sem("hh_hi_done"); hh_lo_done = sem("hh_lo_done"); hh_logits = sem("hh_logits"); h_back = sem("h_back")
        words_ready = sem("words_ready"); x_in = [sem(f"x_in{b}") for b in range(B)]
        ids_in = sem("ids_in"); wa_in = sem("wa_in")
        dst_in = [sem(f"dst_in{s}") for s in range(4)]
        bias_in = [sem(f"bias_in{s}") for s in range(2)]
        w_in = [sem(f"w_in{s}") for s in range(2)]
        stored = [sem(f"stored{s}") for s in range(4)]
        row_in = [sem(f"row_in{s}") for s in range(ROWS)]
        hi_done = sem("hi_done"); lo_done = sem("lo_done"); chunk_used = sem("chunk_used")
        bank_done = sem("bank_done"); evac = sem("evac")
        consts = sem("consts"); own = sem("dve_step"); consts2 = sem("pool_consts_own")
        idsf_ready = sem("idsf_ready"); idsT_ready = sem("idsT_ready"); ids_ready = sem("ids_ready")
        var_ready = sem("var_ready"); rstd_ready = sem("rstd_ready")
        h_pre = sem("h_pre"); h_ready = sem("h_ready"); hT_ready = sem("hT_ready")
        fT_hi_done = sem("fT_hi_done"); fT_lo_done = sem("fT_lo_done")
        member_done = sem("member_done"); edge_done = sem("edge_done")
        lift_ready = sem("lift_ready"); lift_out = sem("lift_out"); lift_in = sem("lift_in"); max_done = sem("max_done")
        pair_ready = sem("pair_ready"); odd_ready = sem("odd_ready"); even_ready = sem("even_ready"); own_act = sem("act_step"); adj_done = sem("adj_done"); adj_full = sem("adj_full")
        adj_ready = sem("adj_ready"); adjT_done = sem("adjT_done"); adjwT_ready = sem("adjwT_ready")
        wsum_ready = sem("wsum_ready"); wdeg_ready = sem("wdeg_ready"); fac_ready = sem("fac_ready")
        mpart_ready = sem("mpart_ready"); me_done = sem("me_done"); arg_ready = sem("arg_ready"); ex_ready = sem("ex_ready")
        adjT_hi_done = sem("adjT_hi_done"); adjT_lo_done = sem("adjT_lo_done")
        hn_hi_done = sem("hn_hi_done"); hn_lo_done = sem("hn_lo_done")
        z_done = sem("z_done"); x_again = sem("x_again")
        x2_step = sem("x2_step"); t_ready = sem("t_ready"); out_ready = sem("out_ready")
        out_stored = [sem(f"out_stored{s}") for s in range(4)]

        TOP, HH, BOT, L1 = UNITS, UNITS + 1, UNITS + 2, UNITS + 3
        first_chunk = {TOP: C_TOP, HH: C_HH, BOT: C_BOT, L1: C_L1}
        done_before = {TOP: 7 * UNITS, HH: 7 * UNITS + 6, BOT: 7 * UNITS + 9, L1: 7 * UNITS + 15}

        def bank_ready(eng, unit, j):
            first, before = first_chunk.get(unit, K * unit), done_before.get(unit, 7 * unit)
            if unit == BOT:
                if j in (1, 7):
                    eng.wait_ge(chunk_used, first + (K if j == 1 else 2 * K))
                else:
                    eng.wait_ge(bank_done, before + max(j, 1))
            elif unit == TOP:
                if j in (1, 7):
                    eng.wait_ge(chunk_used, first + (2 * K if j == 1 else K))
                else:
                    eng.wait_ge(bank_done, before + (j - 1 if j > 1 else 6))
            elif j == (3 if unit == HH else 7):
                eng.wait_ge(chunk_used, first + (2 * K if unit == HH else K))
            else:
                eng.wait_ge(bank_done, before + j + 1)

        MIX = 34

        def pairs_after(i):
            return range(i, i + 1) if i < TE - MIX - 1 else range(i, T // 2)

        def send_lift(eng, c):
            eng.wait_ge(lift_ready, c + 1)
            for a in range(0, P, 32):
                eng.dma_start(lift_row[c, :, a:a + 32], liftT[a:a + CT, c % 2, :]).then_inc(lift_out, 16)

        def fetch_lift(eng, c):
            eng.wait_ge(lift_out, 16 * 4 * (c + 1))
            if c >= 1:
                eng.wait_ge(max_done, 2 * B * c)
            eng.dma_start(lift[:, :], lift_row[c].rearrange("t p -> (t p)").partition_broadcast(P)).then_inc(lift_in, 16)

        block = ctx.enter_context(nc.Block())
        AB = ((0, 0), (0, 1), (1, 0))
        fT, wS, hn, adjT = (fT_hi, fT_lo), (w_hi, w_lo), (hn_hi, hn_lo), (adjT_hi, adjT_lo)

        @block.sync
        def _(sp):
            for b in range(B):
                sp.dma_start(xf[:, b, :], x[b * P:(b + 1) * P, :]).then_inc(x_in[b], 16)
            for a, arr in enumerate((src, dst, edge_w)):
                tgt = ids_row[:, a, :] if a < 2 else ids_rowf[:, a, :]
                for i0, t0, n in RUNS:
                    sp.dma_start(tgt[i0:i0 + n], arr[t0 * P:(t0 + n) * P].rearrange("(t p) -> t p", p=P)).then_inc(ids_in, 16)

            def load(c):
                if c >= 2:
                    sp.wait_ge(lo_done, c - 1)
                sp.dma_start(w_raw[:, c % 2, :], chunk_rows(c)).then_inc(w_in[c % 2], 16)

            def load_bias(n, vec):
                sp.dma_start(bias[:, n % 2, :], vec.partition_broadcast(P)).then_inc(bias_in[n % 2], 16)

            load(0)
            load(1)
            sp.dma_start(wa_rep[:, :], W_a.rearrange("d o -> (d o)").partition_broadcast(P)).then_inc(wa_in, 16)
            sp.dma_start(ba_rep[:, :], b_a.partition_broadcast(P)).then_inc(wa_in, 16)
            load_bias(0, b_ho)
            load_bias(1, b_oo)
            sp.wait_ge(h_ready, B)
            sp.dma_start(h_row.rearrange("(b p) d -> p b d", p=P), xf[:, :, :]).then_inc(h_out, 16)
            for c in range(2, K + 6):
                load(c)
            for u in range(UNITS):
                for j in range(8):
                    e = 8 * u + j
                    sp.wait_ge(evac, e + 1)
                    m, n = j // 2, j % 2
                    sp.dma_start(table[u // 2][u % 2][m * P:(m + 1) * P, n * H:(n + 1) * H],
                                 stage[:, e % 4, :]).then_inc(stored[e % 4], 16)
                if u % 2 == 1:
                    load_bias(2 + u // 2, (b_hn, b_on)[u // 2])
                for c in range(K * (u + 1) + 6, K * (u + 2) + 6):
                    load(c)
            for c in range(C_TOP + 6 + K, C_HH + 6):
                load(c)
            sp.wait_ge(evac, 8 * UNITS + 8)
            load_bias(4, b_hh)
            load_bias(5, b_1)
            for c in range(C_HH + 6, C_BOT + 2):
                load(c)
            fetch_lift(sp, 3)
            for c in range(4, NC):
                send_lift(sp, c)
                fetch_lift(sp, c)
            sp.wait_ge(me_done, 1)
            sp.dma_start(hf[:, :, :], h_row.rearrange("(b p) d -> p b d", p=P)).then_inc(h_back, 16)
            sp.wait_ge(hn_lo_done, B)
            for c in range(C_BOT + 2, C_BOT + 6):
                load(c)
            for b in range(B):
                sp.dma_start(hf[:, b, :], x[b * P:(b + 1) * P, :]).then_inc(x_again, 16)
            for c in range(C_BOT + 6, C_END):
                load(c)
            for j in range(8):
                m, n = j // 2, j % 2
                sp.wait_ge(out_ready, j + 1)
                sp.dma_start(out[m * P:(m + 1) * P, n * H:(n + 1) * H], stage[:, j % 4, :]).then_inc(out_stored[j % 4], 16)
            for s in range(4):
                sp.wait_ge(out_stored[s], 32)

        @block.gpsimd
        def _(pool):
            pool.memset(ident[:, :], 0.0).then_inc(consts2, 1)
            pool.iota(node_no[:, :], [[1, N]], base=0, channel_multiplier=0,
                      allow_small_or_imprecise_dtypes=True).then_inc(consts, 1)
            pool.iota(node_id[:, :], [[P, B]], base=0, channel_multiplier=1,
                      allow_small_or_imprecise_dtypes=True).then_inc(consts, 1)
            pool.memset(ones_f[:, :], 1.0).then_inc(consts, 1)
            pool.memset(zeros[:, :], 0.0).then_inc(consts, 1)
            pool.memset(nhalf[:, :], -0.5).then_inc(consts, 1)
            pool.wait_ge(consts2, 1)
            pool.affine_select(out=ident[:, :], in_=ident[:, :], compare_op=ALU.not_equal, fill=1.0, base=0,
                               pattern=[[-1, P]], channel_multiplier=1).then_inc(consts, 1)
            pool.wait_ge(consts, 6)

            def power(n, dst_t, src_t, ready, done):
                pool.wait_ge(ready, n)
                pool.tensor_tensor(dst_t[:, :], src_t[:, :], nhalf[:, :], ALU.pow).then_inc(done, 1)

            power(1, rstd, veps, var_ready, rstd_ready)
            pool.wait_ge(ids_ready, 1)

            def fetch_src(i, kind, s, lap):
                pool.indirect_dma_start(out=rows[:, s, :], out_offset=None, in_=table[kind][0],
                                        in_offset=bass.IndirectOffsetOnAxis(ap=ids_i[:, 0, i:i + 1], axis=0)
                                        ).then_inc(row_in[s], 16)

            def add_dst(i, kind, s, lap):
                pool.wait_ge(row_in[s], lap * 32 + 16)
                pool.indirect_dma_start(out=rows[:, s, :], out_offset=None, in_=table[kind][1],
                                        in_offset=bass.IndirectOffsetOnAxis(ap=ids_i[:, 1, i:i + 1], axis=0),
                                        compute_op=ALU.add).then_inc(row_in[s], 16)

            def tables_stored(kind):
                for s in range(4):
                    pool.wait_ge(stored[s], 16 * 4 * (kind + 1))

            tables_stored(0)
            AHEAD = 3

            def step(i):
                j = i + AHEAD
                if j < TE:
                    if kind_of(j) != kind_of(j - 1):
                        tables_stored(kind_of(j))
                    if j >= ROWS:
                        pool.wait_ge(edge_done, j - ROWS + 1)
                    fetch_src(j, kind_of(j), j % ROWS, j // ROWS)
                add_dst(i, kind_of(i), i % ROWS, i // ROWS)

            for i in range(AHEAD):
                fetch_src(i, 0, i, 0)
            def fetch_h(side):
                for r in range(TILE_HH):
                    i = TE + r
                    pool.indirect_dma_start(out=h_edge[:, r, :], out_offset=None, in_=h_row,
                                            in_offset=bass.IndirectOffsetOnAxis(ap=ids_i[:, side, i:i + 1], axis=0)
                                            ).then_inc(hh_in[r], 16)

            for i in range(TE):
                if i == 22:
                    for s in range(4):
                        pool.wait_ge(stored[s], 2 * 16 * UNITS)
                    pool.wait_ge(h_out, 16)
                    fetch_h(0)
                if i == 29:
                    pool.wait_ge(hhT_ready, K // 2)
                    fetch_h(1)
                step(i)
            power(1, f_dst, wsum, wsum_ready, fac_ready)
            power(1, f_src, w_out, wdeg_ready, fac_ready)
            for pair in range(T // 2):
                pool.wait_ge(adj_done, T // 2 + pair - (RING - 1))
                t = 2 * pair
                pool.tensor_scalar(pick_src[pair % RING][:, 0, :], node_no[:, :], ids_f[:, 0, t:t + 1], None,
                                   ALU.is_equal).then_inc(even_ready, 1)
            for n in range(B):
                power(2 + n, rstd, veps, var_ready, rstd_ready)

        @block.scalar
        def _(act):
            def dst_rep_load(c):
                i0 = c * CT
                for p0, t0, n in RUNS:
                    a, z = max(i0, p0), min(i0 + CT, p0 + n)
                    if a < z:
                        t = t0 + a - p0
                        act.dma_start(dst_rep[:, c % 4, (a - i0) * P:(z - i0) * P],
                                      dst[t * P:(t + z - a) * P].partition_broadcast(P)).then_inc(dst_in[c % 4], 16)

            for b in range(B):
                act.wait_ge(h_pre, b + 1)
                act.activation(xf[:, b, :], xf[:, b, :], ACT.Relu).then_inc(h_ready, 1)
            for c in range(4):
                dst_rep_load(c)
            for f in range(K):
                act.wait_ge(hT_ready, f + 1)
                act.activation(fT_hi[:, f, :], bank[f][:, :], ACT.Copy).then_inc(fT_hi_done, 1)

            def hi_quad(c0, lap, pe_free):
                for r in range(4):
                    act.wait_ge(w_in[r % 2], lap * 32 + 16 * (r // 2 + 1))
                    if pe_free:
                        act.wait_ge(chunk_used, c0 + (r - 3))
                    act.activation(w_hi[:, r, :], w_raw[:, r % 2, :], ACT.Copy).then_inc(hi_done, 1)

            def evacuate(u):
                for j in range(8):
                    e = 8 * u + j
                    bank_ready(act, u, j)
                    if e >= 4:
                        act.wait_ge(stored[e % 4], 16 * (e // 4))
                    act.activation(stage[:, e % 4, :], bank[j][:, :], ACT.Copy).then_inc(evac, 1)

            hi_quad(0, 0, False)
            for c in range(4, NC):
                act.wait_ge(member_done, c - 3)
                dst_rep_load(c)
            for u in range(UNITS):
                with act.Fori(2 * u + 1, 2 * u + 3) as q:
                    hi_quad(q * 4, q, True)
                if u % 2 == 0:
                    evacuate(u)
            send_lift(act, 0)
            with act.Fori(2 * UNITS + 1, 2 * UNITS + 3) as q:
                hi_quad(q * 4, q, True)
            fetch_lift(act, 0)
            send_lift(act, 1)
            hi_quad(C_HH - 4, C_HH // 4 - 1, True)

            def high_of_edges(side):
                for g in range(K // 2):
                    act.wait_ge(hhT_ready, side * (K // 2) + g + 1)
                    act.activation(fT_hi[:, 2 * g:2 * g + 2, side * 2 * P:(side + 1) * 2 * P],
                                   bank[4 + g].rearrange("p (f e) -> p f e", f=2), ACT.Copy).then_inc(hh_hi_done, 1)

            hi_quad(C_HH, C_HH // 4, True)
            act.wait_ge(chunk_used, C_HH)
            high_of_edges(0)
            hi_quad(C_HH + 4, C_HH // 4 + 1, True)
            high_of_edges(1)
            fetch_lift(act, 1)
            send_lift(act, 2)
            with act.Fori(C_HH // 4 + 2, C_HH // 4 + 4) as q:
                hi_quad(q * 4, q, True)
            fetch_lift(act, 2)
            send_lift(act, 3)
            mine = [0]

            def pick_odd(pair, slot, waits):
                if waits is not None:
                    act.wait_ge(adj_done, waits)
                t = pair * 2 + 1
                gap = pick_src[slot][:, 1, :].bitcast(F16)
                act.activation(gap, node_no[:, :], ACT.Abs, bias=ids_f[:, 0, t:t + 1], scale=-1.0).then_inc(own_act, 1)
                mine[0] += 1
                act.wait_ge(own_act, mine[0])
                act.activation(pick_src[slot][:, 1, :], gap, ACT.Relu, bias=ones_f[:, 0:1], scale=-1.0
                               ).then_inc(odd_ready, 1)

            for t in range(MIX, TE):
                for pair in pairs_after(t - MIX):
                    if pair == 0:
                        act.wait_ge(hh_logits, TILE_HH)
                    pick_odd(pair, pair % RING, pair - (RING - 1) if pair >= RING else None)
            act.wait_ge(arg_ready, 1)
            act.activation(ex[:, :], me[:, :], ACT.Exp, scale=-1.0).then_inc(ex_ready, 1)
            for pair in range(T // 2):
                pick_odd(pair, pair % RING, T // 2 + pair - (RING - 1))
                if pair % CT == CT - 1:
                    act.wait_ge(h_back, 16)
                    b = pair // CT
                    act.activation(hn_hi[:, b, :], hf[:, b, :], ACT.Copy).then_inc(hn_hi_done, 1)
            for s in range(B):
                act.wait_ge(adjT_done, B + s + 1)
                act.activation(adjT_hi[:, s, :], bank[4 + s][:, :], ACT.Copy).then_inc(adjT_hi_done, 1)
            hi_quad(C_BOT, C_BOT // 4, True)
            for f in range(K):
                act.wait_ge(z_done, f + 1)
                act.activation(fT_hi[:, f, :], bank[f][:, :], ACT.Copy).then_inc(fT_hi_done, 1)
            for s in range(B):
                act.activation(adjT_hi[:, s, :], adjwT[:, s, :], ACT.Copy).then_inc(adjT_hi_done, 1)
            with act.Fori(C_BOT // 4 + 1, C_L1 // 4) as q:
                hi_quad(q * 4, q, True)
            for b in range(B):
                act.wait_ge(h_pre, B + b + 1)
                act.activation(hn_hi[:, b, :], hf[:, b, :], ACT.Relu).then_inc(hn_hi_done, 1)
            hi_quad(C_L1, C_L1 // 4, True)
            for f in range(K):
                act.wait_ge(z_done, K + f + 1)
                act.activation(fT_hi[:, f, :], bank[f][:, :], ACT.Copy).then_inc(fT_hi_done, 1)
            hi_quad(C_L1 + 4, C_L1 // 4 + 1, True)

        @block.vector
        def _(dve):
            step = Step(dve, own)

            def build_member(c):
                dve.wait_ge(dst_in[c % 4], 16 * dst_loads(c))
                for b in range(B):
                    ins = dve.tensor_scalar(member[:, b, c * CE:(c + 1) * CE], dst_rep[:, c % 4, :],
                                            node_id[:, b:b + 1], 0.0, ALU.is_equal, ALU.add,
                                            accum_out=count[:, b, c:c + 1])
                ins.then_inc(member_done, 1)

            def dst_loads(c):
                total = 0
                for cc in range(c % 4, c + 1, 4):
                    for p0, t0, n in RUNS:
                        total += max(cc * CT, p0) < min(cc * CT + CT, p0 + n)
                return total

            def norm_stats(blocks, arrived=None):
                for b in blocks:
                    if arrived is not None:
                        dve.wait_ge(arrived[b], 16)
                    for n in range(2):
                        ins = dve.bn_stats(stats[:, b, n, :], xf[:, b, n * H:(n + 1) * H])
                    step(ins)
                    ins = dve.bn_aggr(mv[:, b, :], stats[:, b, :, :])
                    step(ins)

            norm_stats(range(B), x_in)
            dve.tensor_scalar(veps[:, :], mv[:, :, 1], EPS, None, ALU.add).then_inc(var_ready, 1)
            dve.wait_ge(rstd_ready, 1)
            for b in range(B):
                dve.tensor_scalar(xf[:, b, :], xf[:, b, :], mv[:, b, 0:1], rstd[:, b:b + 1], ALU.subtract,
                                  ALU.mult).then_inc(h_pre, 1)
            dve.wait_ge(ids_in, 16 * 3 * len(RUNS))
            step(dve.tensor_copy(ids_rowf[:, 0:2, :], ids_row[:, 0:2, :]))
            dve.wait_ge(consts, 6)
            block_no = ids_row[:, 0, :].bitcast(F32)
            step(dve.tensor_scalar(block_no, ids_rowf[:, 1, :], float(P), None, ALU.is_ge))
            for b in range(2, B):
                step(dve.scalar_tensor_tensor(block_no, ids_rowf[:, 1, :], float(b * P), block_no, ALU.is_ge, ALU.add))
            dve.tensor_reduce(tile_lo[:, 0:1], block_no, AX.X, ALU.min)
            dve.tensor_reduce(tile_lo[:, 1:2], block_no, AX.X, ALU.max).then_inc(idsf_ready, 1)
            dve.wait_ge(idsT_ready, 1)
            step(dve.tensor_copy(ids_f[:, :, :], bank[0][:, 0:3 * T].rearrange("p (a t) -> p a t", a=3)))
            dve.tensor_copy(ids_i[:, :, :], ids_f[:, 0:2, :]).then_inc(ids_ready, 1)
            for k, op in enumerate((ALU.min, ALU.max)):
                step(dve.tensor_reduce(pair_row[:, k, :], bank[0][0:1, (3 + k) * T:(4 + k) * T].rearrange(
                    "o (p r) -> o p r", r=2), AX.X, op))
            for k in range(4):
                ins = dve.memset(nibble[:, :, k:k + 1], float(16 ** k))
            step(ins)
            step(dve.scalar_tensor_tensor(pair_row[:, 2, :], pair_row[:, 1, :], 4.0, pair_row[:, 0, :], ALU.mult, ALU.add))
            step(dve.tensor_tensor(nibble[:, :, :], nibble[:, :, :], pair_row[:, 2, :].rearrange("o (w k) -> o w k", k=4),
                                   ALU.mult))
            step(dve.tensor_reduce(pair_row[:, 0, 0:T // 8], nibble[:, :, :], AX.X, ALU.add))
            dve.tensor_copy(pair_word[:, :], pair_row[:, 0, 0:T // 8]).then_inc(words_ready, 1)

            def split3(parts, whole, n):
                src_ap = whole
                for k in range(3):
                    step(dve.tensor_copy(part16[:, :], src_ap))
                    step(dve.tensor_copy(parts[:, k, :], part16[:, :]))
                    if k < 2:
                        step(dve.tensor_tensor(rest[:, :], src_ap, parts[:, k, :], ALU.subtract))
                        src_ap = rest[:, :]

            for f in range(K):
                dve.wait_ge(fT_hi_done, f + 1)
                dve.tensor_tensor(fT_lo[:, f, :], bank[f][:, :], fT_hi[:, f, :].bitcast(F32), ALU.subtract
                                  ).then_inc(fT_lo_done, 1)

            def lo(c0, r, pe_free):
                dve.wait_ge(hi_done, c0 + (r + 1))
                if pe_free:
                    dve.wait_ge(chunk_used, c0 + (r - 3))
                dve.tensor_tensor(w_lo[:, r, :], w_raw[:, r % 2, :], w_hi[:, r, :].bitcast(F32), ALU.subtract
                                  ).then_inc(lo_done, 1)

            def edge(i):
                r = i % ROWS
                dve.wait_ge(row_in[r], i // ROWS * 32 + 32)
                dve.scalar_tensor_tensor(rows[:, r, :], rows[:, r, :], 0.0, wa_rep[:, :], ALU.max, ALU.mult,
                                         accum_out=logit[:, i:i + 1]).then_inc(edge_done, 1)

            def lift_chunk(c):
                a, z = c * CT, (c + 1) * CT
                dve.wait_ge(edge_done, min(z, TE))
                if c == NC - 1:
                    dve.wait_ge(hh_logits, TILE_HH)
                step(dve.tensor_scalar(lb[:, a:z], logit[:, a:z], ba_rep[:, 0:1], None, ALU.add))
                step(dve.tensor_scalar(lifted[:, c % 2, 0:CT], lb[:, a:z], BIG, None, ALU.add))
                if c >= 2:
                    dve.wait_ge(lift_out, 16 * 4 * (c - 1))
                dve.transpose(liftT[:, c % 2, :], lifted[:, c % 2, :]).then_inc(lift_ready, 1)

            def chunk_max(c):
                dve.wait_ge(lift_in, 16 * (c + 1))
                for n in range(2 * B):
                    b, h = n // 2, n % 2
                    a, z = h * CE // 2, (h + 1) * CE // 2
                    if c or n:
                        dve.wait_ge(max_done, 2 * B * c + n)
                    dve.tensor_tensor_reduce(masked[:, :], lift[:, a:z], member[:, b, c * CE + a:c * CE + z], 1.0, 0.0,
                                             ALU.mult, ALU.max, cmax[:, b, 2 * c + h:2 * c + h + 1]).then_inc(max_done, 1)

            def evacuate(u):
                kind = u // 2
                dve.wait_ge(bias_in[kind % 2], 16 * (kind // 2 + 1))
                for j in range(8):
                    e = 8 * u + j
                    bank_ready(dve, u, j)
                    dve.wait_ge(stored[e % 4], 16 * (e // 4))
                    n = j % 2
                    dve.tensor_tensor(stage[:, e % 4, :], bank[j][:, :], bias[:, kind % 2, n * H:(n + 1) * H],
                                      ALU.add).then_inc(evac, 1)

            for r in range(4):
                lo(0, r, False)
            split3(w_part, ids_f[:, 2, :], T)
            dve.memset(w_col[:, :, 0:1], 1.0)
            step(dve.tensor_copy(w_col[:, :, 1:4], w_part.rearrange("p k t -> p t k")))
            step(dve.memset(lifted[:, :, :], 0.0))
            dve.wait_ge(words_ready, 1)
            for c in range(4):
                build_member(c)
            dve.wait_ge(wa_in, 32)
            for u in range(UNITS + 1):
                if u < 2:
                    with dve.Fori(2 * u + 1, 2 * u + 3) as q:
                        for r in range(4):
                            lo(q * 4, r, True)
                else:
                    for c in range(8 * u + 4, 8 * u + 12):
                        lo(c // 4 * 4, c % 4, True)
                        edge(c - 8 * u - 4 + 8 * (u - 2))
                if u < UNITS and u % 2 == 1:
                    evacuate(u)
                if u == 0:
                    for c in range(4, NC):
                        build_member(c)
                    dve.wait_ge(member_done, NC)
                    step(dve.tensor_reduce(deg_in[:, :], count[:, :, :], AX.X, ALU.add))
                if u >= 2:
                    lift_chunk(u - 2)
            at_edge = 8 * (UNITS - 1)

            dve.wait_ge(bias_in[1], 32)
            dve.wait_ge(bias_in[0], 32)
            dve.wait_ge(h_out, 16)

            def keep_top(banks):
                for j in banks:
                    m, n = j // 2, j % 2
                    bank_ready(dve, TOP, j)
                    dve.tensor_tensor(xf[:, m, n * H:(n + 1) * H], bank[j][:, :],
                                      bias[:, 0 if m < BLOCK_H else 1, n * H:(n + 1) * H], ALU.add).then_inc(evac, 1)

            def low_of_edges(side):
                for g in range(K // 2):
                    dve.wait_ge(hh_hi_done, side * (K // 2) + g + 1)
                    part = (slice(None), slice(2 * g, 2 * g + 2), slice(side * 2 * P, (side + 1) * 2 * P))
                    dve.tensor_tensor(fT_lo[part], bank[4 + g].rearrange("p (f e) -> p f e", f=2),
                                      fT_hi[part].bitcast(F32), ALU.subtract).then_inc(hh_lo_done, 1)

            def lo_and_edges(c0, i):
                for r in range(4):
                    lo(c0, r, True)
                    if r % 2 == 1:
                        edge(i + r // 2)

            keep_top(range(2, 8))
            lo_and_edges(C_HH - 4, at_edge)
            for r in range(4):
                lo(C_HH, r, True)
            keep_top(range(2))
            low_of_edges(0)
            chunk_max(0)
            edge(at_edge + 2)
            edge(at_edge + 3)
            lo_and_edges(C_HH + 4, at_edge + 4)
            low_of_edges(1)
            lo_and_edges(C_HH + 8, at_edge + 6)
            lift_chunk(3)
            chunk_max(1)
            lo_and_edges(C_HH + 12, at_edge + 8)
            dve.wait_ge(bias_in[0], 48)
            for r in range(TILE_HH):
                for n in range(2):
                    bank_ready(dve, HH, 2 * r + n)
                    ins = dve.tensor_tensor(h_edge[:, r, n * H:(n + 1) * H], bank[2 * r + n][:, :],
                                            bias[:, 0, n * H:(n + 1) * H], ALU.add)
                step(ins)
                dve.scalar_tensor_tensor(h_edge[:, r, :], h_edge[:, r, :], 0.0, wa_rep[:, :], ALU.max, ALU.mult,
                                         accum_out=logit[:, TE + r:TE + r + 1]).then_inc(hh_logits, 1)
            chunk_max(2)

            def spread(word, pair, parts, first_pair):
                k, slot = pair % 4, pair % RING
                if first_pair + pair >= RING:
                    dve.wait_ge(adj_done, first_pair + pair - (RING - 1))
                lo_b, hi_b = dve.snap((word >> (4 * k)) & 3), dve.snap((word >> (4 * k + 2)) & 3)
                with dve.Fori(lo_b, hi_b + 1) as b:
                    for r in range(2):
                        t = pair * 2 + r
                        dve.scalar_tensor_tensor(pick_dst[slot][:, r, :, bass.ds(b * P, P)],
                                                 node_no[:, None, bass.ds(b * P, P)].broadcast_to([P, 3, P]),
                                                 ids_f[:, 1, t:t + 1], parts[:, :, t:t + 1].broadcast_to([P, 3, P]),
                                                 ALU.is_equal, ALU.mult)
                if first_pair == 0:
                    ins = dve.tensor_scalar(pick_src[slot][:, 0, :], node_no[:, :], ids_f[:, 0, 2 * pair:2 * pair + 1],
                                            None, ALU.is_equal)
                else:
                    ins = dve.memset(pair_end[:, pair:pair + 1], 0.0)
                ins.then_inc(pair_ready, 1)

            def pair_blocks(q):
                return dve.value_load(pair_word[0:1, bass.ds(q, 1)], min_val=0, max_val=16 ** 4 - 1)

            for t in range(MIX, TE):
                edge(t)
                if t % CT == CT - 1 or t == TE - 1:
                    lift_chunk(t // CT)
                for pair in pairs_after(t - MIX):
                    if pair % 4 == 0:
                        word = pair_blocks(pair // 4)
                    spread(word, pair, w_part, 0)
                if t == MIX + 2 or t > MIX + 2 and t % CT == 3:
                    chunk_max((t - 8) // CT)
            chunk_max(7)
            dve.wait_ge(max_done, 2 * B * NC)
            step(dve.tensor_reduce(mx[:, :], cmax[:, :, :], AX.X, ALU.max))
            left = mx
            for k in range(3):
                ins = dve.tensor_copy(mpart[:, :, k], left[:, :])
                if k == 2:
                    ins.then_inc(mpart_ready, 1)
                else:
                    step(ins)
                    step(dve.tensor_tensor(mrest[:, :], left[:, :], mpart[:, :, k], ALU.subtract))
                    left = mrest
            dve.wait_ge(adj_full, 1)
            for b in range(B):
                ins = dve.tensor_reduce(wsum[:, b:b + 1], bank[b][:, :], AX.X, ALU.add)
            step(ins)
            step(dve.tensor_scalar(wsum[:, :], wsum[:, :], TINY, None, ALU.max))
            step(dve.tensor_scalar(deg_in[:, :], deg_in[:, :], 1.0, None, ALU.max))
            step(dve.tensor_tensor(mrest[:, :], wsum[:, :], deg_in[:, :], ALU.mult))
            dve.tensor_copy(wsum[:, :], mrest[:, :]).then_inc(wsum_ready, 1)
            sums = bank[4][:, 0:4 * B].rearrange("p (b k) -> p b k", k=4)
            step(dve.tensor_scalar(deg_out[:, :], sums[:, :, 0], 1.0, None, ALU.max))
            step(dve.tensor_reduce(mrest[:, :], sums[:, :, 1:4], AX.X, ALU.add))
            step(dve.tensor_scalar(mrest[:, :], mrest[:, :], TINY, None, ALU.max))
            dve.tensor_tensor(w_out[:, :], mrest[:, :], deg_out[:, :], ALU.mult).then_inc(wdeg_ready, 1)
            dve.wait_ge(fac_ready, 1)
            for b in range(B):
                dve.tensor_scalar(adj[:, b, :], bank[b][:, :], f_dst[:, b:b + 1], None, ALU.mult).then_inc(adj_ready, 1)
            dve.wait_ge(me_done, 1)
            step(dve.tensor_reduce(me[:, :], bank[5][:, 0:3 * T].rearrange("p (t k) -> p t k", k=3), AX.X, ALU.add))
            step(dve.tensor_scalar(rest[:, :], me[:, :], -BIG, None, ALU.add))
            dve.tensor_tensor(me[:, :], rest[:, :], lb[:, :], ALU.subtract).then_inc(arg_ready, 1)
            for s in range(B):
                dve.wait_ge(adjT_done, s + 1)
                dve.tensor_copy(adjwT[:, s, :], bank[4 + s][:, :]).then_inc(adjwT_ready, 1)
            dve.wait_ge(ex_ready, 1)
            split3(e_part, ex[:, :], T)
            for b in range(B):
                for q in range(2 * b, 2 * b + 2):
                    word = pair_blocks(q)
                    for k in range(4):
                        spread(word, q * 4 + k, e_part, T // 2)
                dve.wait_ge(hn_hi_done, b + 1)
                dve.tensor_tensor(hn_lo[:, b, :], hf[:, b, :], hn_hi[:, b, :].bitcast(F32), ALU.subtract
                                  ).then_inc(hn_lo_done, 1)
            dve.wait_ge(adj_full, 2)
            for b in range(B):
                ins = dve.tensor_reduce(wsum[:, b:b + 1], bank[b][:, :], AX.X, ALU.add)
            step(ins)
            step(dve.tensor_scalar(wsum[:, :], wsum[:, :], TINY, None, ALU.max))
            step(dve.reciprocal(rden[:, :], wsum[:, :]))
            for b in range(B):
                dve.tensor_scalar(adj[:, b, :], bank[b][:, :], rden[:, b:b + 1], None, ALU.mult).then_inc(adj_ready, 1)

            def low_of(dst_t, s, psum, hi_t, hi_sem, hi_n, done):
                dve.wait_ge(hi_sem, hi_n)
                dve.tensor_tensor(dst_t[:, s, :], psum, hi_t[:, s, :].bitcast(F32), ALU.subtract).then_inc(done, 1)

            for s in range(B):
                low_of(adjT_lo, s, bank[4 + s][:, :], adjT_hi, adjT_hi_done, s + 1, adjT_lo_done)
            for r in range(4):
                lo(C_BOT, r, True)
            for f in range(K):
                low_of(fT_lo, f, bank[f][:, :], fT_hi, fT_hi_done, K + f + 1, fT_lo_done)
            for s in range(B):
                low_of(adjT_lo, s, adjwT[:, s, :], adjT_hi, adjT_hi_done, B + s + 1, adjT_lo_done)
            with dve.Fori(C_BOT // 4 + 1, C_L1 // 4 - 1) as q:
                for r in range(4):
                    lo(q * 4, r, True)
            dve.wait_ge(x_again, 16 * B)
            dve.wait_ge(fac_ready, 2)

            def second_x(m):
                for n in range(2):
                    j, a, z = 2 * m + n, n * H, (n + 1) * H
                    bank_ready(dve, BOT, j)
                    step(dve.tensor_tensor(xf[:, m, a:z], bank[j][:, :], xf[:, m, a:z], ALU.add))
                    dve.scalar_tensor_tensor(xf[:, m, a:z], xf[:, m, a:z], 0.0, hf[:, m, a:z], ALU.max,
                                             ALU.add).then_inc(x2_step, 1)
                dve.wait_ge(x2_step, 2 * m + 2)
                norm_stats((m,))

            def root(m):
                dve.tensor_scalar(veps[:, :], mv[:, :, 1], EPS, None, ALU.add).then_inc(var_ready, 1)

            def second_h(m):
                dve.wait_ge(rstd_ready, 2 + m)
                step(dve.tensor_tensor(rstd[:, m:m + 1], rstd[:, m:m + 1], f_src[:, m:m + 1], ALU.mult))
                dve.tensor_scalar(hf[:, m, :], xf[:, m, :], mv[:, m, 0:1], rstd[:, m:m + 1], ALU.subtract,
                                  ALU.mult).then_inc(h_pre, 1)

            def second_h_lo(m):
                dve.wait_ge(hn_hi_done, B + m + 1)
                dve.scalar_tensor_tensor(hn_lo[:, m, :], hf[:, m, :], 0.0, hn_hi[:, m, :].bitcast(F32), ALU.max,
                                         ALU.subtract).then_inc(hn_lo_done, 1)

            second_x(0)
            root(0)
            for r in range(4):
                lo(C_L1 - 4, r, True)
            second_h(0)
            for m in range(1, B):
                second_x(m)
                root(m)
                second_h_lo(m - 1)
                second_h(m)
            second_h_lo(B - 1)
            for r in range(4):
                lo(C_L1, r, True)
            for f in range(K):
                low_of(fT_lo, f, bank[f][:, :], fT_hi, fT_hi_done, 2 * K + f + 1, fT_lo_done)
            for r in range(4):
                lo(C_L1 + 4, r, True)
            dve.wait_ge(bias_in[1], 48)
            for j in range(8):
                m, n = j // 2, j % 2
                a, z = n * H, (n + 1) * H
                bank_ready(dve, L1, j)
                if j >= 4:
                    dve.wait_ge(out_stored[j % 4], 16)
                step(dve.tensor_tensor(stage[:, j % 4, :], bank[j][:, :], bias[:, 1, a:z], ALU.add))
                dve.scalar_tensor_tensor(stage[:, j % 4, :], stage[:, j % 4, :], 0.0, xf[:, m, a:z], ALU.max,
                                         ALU.add).then_inc(out_ready, 1)

        @block.tensor
        def _(pe):
            pe.wait_ge(consts, 6)
            pe.wait_ge(idsf_ready, 1)
            for a in range(3):
                ins = pe.transpose(bank[0][:, a * T:(a + 1) * T], ids_rowf[:, a, :], ident[0:T, 0:T])
            for k in range(2):
                ins = pe.transpose(bank[0][0:1, (3 + k) * T:(4 + k) * T], tile_lo[:, k:k + 1], ident[0:T, 0:T])
            ins.then_inc(idsT_ready, 1)
            pe.wait_ge(h_ready, B)
            pe.wait_ge(words_ready, 1)
            pe.wait_ge(ids_ready, 1)
            for f in range(K):
                for b in range(B):
                    ins = pe.transpose(bank[f][:, b * P:(b + 1) * P], xf[:, b, f * P:(f + 1) * P], ident[:, :])
                ins.then_inc(hT_ready, 1)

            def chunk(c, k, slot, banks, evac_wait):
                pe.wait_ge(lo_done, c + 1)
                for j in banks:
                    if k == 0 and evac_wait is not None:
                        pe.wait_ge(evac, evac_wait + (j + 1))
                    m, n = j // 2, j % 2
                    for p, (a, b) in enumerate(AB):
                        ins = pe.matmul(bank[j][:, :], fT[a][:, k, m * P:(m + 1) * P],
                                        wS[b][:, slot, n * H:(n + 1) * H],
                                        start=(k == 0 and p == 0), stop=(k == K - 1 and p == 2))
                    if k == K - 1 and j != banks[-1]:
                        ins.then_inc(bank_done, 1)
                ins.then_inc(chunk_used, 1)

            ALL = range(8)
            pe.wait_ge(fT_lo_done, K)
            for k in range(K):
                chunk(k, k, k % 4, ALL, None)
            with pe.Fori(1, UNITS) as u:
                for k in range(K):
                    chunk(u * K + k, k, k % 4, ALL, u * 8 - 8)
            for k in range(K):
                chunk(C_TOP + k, k, k % 4, range(2, 8), 8 * UNITS - 8)
            for k in range(K):
                chunk(C_TOP + K + k, k, k % 4, range(2), 8 * UNITS - 8)

            def transpose_edges(side):
                for r in range(TILE_HH):
                    pe.wait_ge(hh_in[r], 16 * (side + 1))
                for g in range(K // 2):
                    if side == 0:
                        pe.wait_ge(evac, 8 * UNITS + g + 3)
                    else:
                        pe.wait_ge(hh_lo_done, g + 1)
                    for i in range(2):
                        for r in range(TILE_HH):
                            f = 2 * g + i
                            ins = pe.transpose(bank[4 + g][:, (2 * i + r) * P:(2 * i + r + 1) * P],
                                               h_edge[:, r, f * P:(f + 1) * P], ident[:, :])
                    ins.then_inc(hhT_ready, 1)

            transpose_edges(0)
            pe.wait_ge(evac, 8 * UNITS + 8)
            for k in range(2 * K):
                if k == K - 2:
                    transpose_edges(1)
                side = k // K
                pe.wait_ge(hh_lo_done, side * (K // 2) + (k % K) // 2 + 1)
                pe.wait_ge(lo_done, C_HH + k + 1)
                for j in range(2 * TILE_HH):
                    r, n = j // 2, j % 2
                    for p, (a, b) in enumerate(AB):
                        ins = pe.matmul(bank[j][:, :], fT[a][:, k % K, (2 * side + r) * P:(2 * side + r + 1) * P],
                                        wS[b][:, k % 4, n * H:(n + 1) * H],
                                        start=(k == 0 and p == 0), stop=(k == 2 * K - 1 and p == 2))
                    if k == 2 * K - 1 and j < 2 * TILE_HH - 1:
                        ins.then_inc(bank_done, 1)
                ins.then_inc(chunk_used, 1)

            def adj_clear():
                for b in range(B):
                    pe.matmul(bank[b][:, :], zeros[:, :], node_no[:, :], start=True, stop=True)
                pe.matmul(bank[4][:, 0:4 * B], zeros[:, :], node_no[:, 0:4 * B], start=True, stop=True)

            def adj_close(deg):
                if deg:
                    pe.matmul(bank[4][:, 0:4 * B], zeros[:, :], node_no[:, 0:4 * B], start=False, stop=True,
                              skip_group_check=True)
                for b in range(B):
                    ins = pe.matmul(bank[b][:, :], zeros[:, :], node_no[:, :], start=False, stop=True,
                                    skip_group_check=True)
                ins.then_inc(adj_full, 1)

            def adj_sum(first_pair, deg):
                for pair in range(T // 2):
                    k, slot = pair % 4, pair % RING
                    if k == 0:
                        word = pe.value_load(pair_word[0:1, pair // 4:pair // 4 + 1], min_val=0, max_val=16 ** 4 - 1)
                    lo, hi = pe.snap((word >> (4 * k)) & 3), pe.snap((word >> (4 * k + 2)) & 3)
                    pe.wait_ge(pair_ready, first_pair + pair + 1)
                    pe.wait_ge(odd_ready, first_pair + pair + 1)
                    if not deg:
                        pe.wait_ge(even_ready, pair + 1)
                    if deg:
                        for r in range(2):
                            for b in range(B):
                                pe.matmul(bank[4][:, 4 * b:4 * b + 4], pick_src[slot][:, r, b * P:(b + 1) * P],
                                          w_col[:, 2 * pair + r, :], start=False, stop=True, skip_group_check=True)
                    with pe.Fori(lo, hi + 1) as b:
                        for r in range(2):
                            for p in range(3):
                                pe.matmul(banks[:, bass.ds(b * H, H)], pick_dst[slot][:, r, p, bass.ds(b * P, P)],
                                          pick_src[slot][:, r, :], start=False, stop=True, skip_group_check=True)
                    pe.matmul(bank[4][:, 0:B], zeros[:, :], node_no[:, 0:B], start=False, stop=True,
                              skip_group_check=True).then_inc(adj_done, 1)

            def transpose_adj(n):
                for b in range(B):
                    pe.wait_ge(adj_ready, n + b + 1)
                for s in range(B):
                    for b in range(B):
                        ins = pe.transpose(bank[4 + s][:, b * P:(b + 1) * P], adj[:, b, s * P:(s + 1) * P], ident[:, :])
                    ins.then_inc(adjT_done, 1)

            pe.wait_ge(hh_logits, TILE_HH)
            pe.wait_ge(hh_lo_done, K)
            adj_clear()
            adj_sum(0, True)
            adj_close(True)
            pe.wait_ge(mpart_ready, 1)
            for t in range(T):
                for b in range(B):
                    ins = pe.matmul(bank[5][:, 3 * t:3 * t + 3], member[:, b, t * P:(t + 1) * P], mpart[:, b, :],
                                    start=(b == 0), stop=(b == B - 1))
            ins.then_inc(me_done, 1)
            pe.wait_ge(arg_ready, 1)
            pe.wait_ge(wdeg_ready, 1)
            transpose_adj(0)
            pe.wait_ge(adjwT_ready, B)
            adj_clear()
            adj_sum(T // 2, False)
            adj_close(False)
            transpose_adj(B)

            def features(order, n_adj, n_hn, first_layer):
                for i, s in enumerate(order):
                    pe.wait_ge(adjT_lo_done, n_adj + (s + 1 if i == 0 or n_adj == 0 else B))
                    pe.wait_ge(hn_lo_done, n_hn + i + 1)
                    for f in range(K):
                        if i == 0 and first_layer and f >= 4:
                            pe.wait_ge(adjT_lo_done, f - 3)
                        if i == 0 and not first_layer:
                            pe.wait_ge(x2_step, f + 1)
                        for p, (a, b) in enumerate(AB):
                            ins = pe.matmul(bank[f][:, :], hn[a][:, s, f * P:(f + 1) * P], adjT[b][:, s, :],
                                            start=(i == 0 and p == 0), stop=(i == B - 1 and p == 2))
                        if i == B - 1:
                            ins.then_inc(z_done, 1)

            def products(c0, blocks):
                banks = range(2 * blocks[0], 2 * blocks[-1] + 2)
                for k in range(K // 2):
                    chunk(c0 + k, k, k % 4, banks, None)
                for m in blocks:
                    for k in range(K // 2, K):
                        if m == blocks[0]:
                            pe.wait_ge(lo_done, c0 + k + 1)
                        for n in range(2):
                            for p, (a, b) in enumerate(AB):
                                ins = pe.matmul(bank[2 * m + n][:, :], fT[a][:, k, m * P:(m + 1) * P],
                                                wS[b][:, k % 4, n * H:(n + 1) * H],
                                                start=False, stop=(k == K - 1 and p == 2))
                            if k == K - 1 and 2 * m + n != banks[-1]:
                                ins.then_inc(bank_done, 1)
                        if m == blocks[-1]:
                            ins.then_inc(chunk_used, 1)

            features(range(B), 0, 0, True)
            pe.wait_ge(fT_lo_done, 2 * K)
            for k in range(K):
                chunk(C_BOT + k, k, k % 4, range(2), None)
            products(C_BOT + K, range(BLOCK_H, B))
            pe.wait_ge(adjT_lo_done, 2 * B)
            features(range(B), B, B, False)
            pe.wait_ge(fT_lo_done, 3 * K)
            products(C_L1, range(B))


_INS = ["x", "src", "dst", "edge_weight", "L0_gnn_W_hh", "L0_gnn_b_hh", "L0_gnn_W_oo", "L0_gnn_b_oo", "L0_gnn_W_ho",
        "L0_gnn_b_ho", "L0_gnn_W_a", "L0_gnn_b_a", "L0_gnn_W_hn", "L0_gnn_b_hn", "L0_gnn_W_on", "L0_gnn_b_on",
        "L1_gnn_W", "L1_gnn_b"]


def kernel(**inputs):
    import numpy as _np
    import concourse.bacc as _bacc
    from concourse import mybir as _mybir
    from concourse.bass_utils import run_bass_kernel_spmd as _run

    nc = _bacc.Bacc("TRN2", target_bir_lowering=False, num_devices=1)
    arrays, args = {}, []
    for name in _INS:
        a = _np.ascontiguousarray(inputs[name])
        arrays[f"in_{name}_dram"] = a
        args.append(nc.dram_tensor(f"in_{name}_dram", a.shape, _mybir.dt.from_np(a.dtype), kind="ExternalInput").ap())
    out = nc.dram_tensor("out_0_dram", inputs["x"].shape, _mybir.dt.float32, kind="ExternalOutput").ap()
    build(nc, *args, out)
    r = _run(nc, [arrays], core_ids=[0])
    return r.results[0]["out_0_dram"]
```

```python
from contextlib import ExitStack

import concourse.bass as bass
from concourse import mybir
from concourse.alu_op_type import AluOpType as ALU

ACT = mybir.ActivationFunctionType
AX = mybir.AxisListType
F32, F32R, BF16, F16 = mybir.dt.float32, mybir.dt.float32r, mybir.dt.bfloat16, mybir.dt.float16
I32 = mybir.dt.int32

P = 128
EPS = 1e-5
TINY = 1e-30
BIG = float(2 ** 20)

TILE_HH, TILE_OO = 2, 12
BLOCK_H = 1


def tile_order(T):
    first = 16
    runs = [(0, first, T - first)]
    runs.append((T - first, TILE_OO, first - TILE_OO))
    runs.append((T - TILE_OO, TILE_HH, TILE_OO - TILE_HH))
    runs.append((T - TILE_HH, 0, TILE_HH))
    return runs


class Step:

    def __init__(self, eng, sem):
        self.eng, self.sem, self.n = eng, sem, 0

    def __call__(self, ins):
        self.n += 1
        ins.then_inc(self.sem, 1)
        self.eng.wait_ge(self.sem, self.n)


def build(nc, x, src, dst, edge_w, W_hh, b_hh, W_oo, b_oo, W_ho, b_ho, W_a, b_a, W_hn, b_hn, W_on, b_on,
          W_1, b_1, out):
    N, D = x.shape
    E = src.shape[0]
    B, K, T = N // P, D // P, E // P
    H = D // 2
    CT = 8
    NC = T // CT
    CE = CT * P
    RUNS = tile_order(T)
    TE = T - TILE_HH
    kind_of = lambda i: 0 if i < T - TILE_OO else 1

    kinds = [(W_ho, b_ho), (W_oo, b_oo)]
    UNITS = 2 * len(kinds)
    C_TOP = K * UNITS
    C_HH = C_TOP + 2 * K
    C_BOT = C_HH + 2 * K
    C_L1 = C_BOT + 2 * K
    C_END = C_L1 + K

    def chunk_rows(c):
        if c < C_TOP:
            u, k = c // K, c % K
            w, row = kinds[u // 2][0], (u % 2) * D + k * P
        elif C_HH <= c < C_BOT:
            w, row = W_hh, (c - C_HH) * P
        elif c < C_L1:
            bottom = c >= C_BOT
            q, k = (c - (C_BOT if bottom else C_TOP)) // K, c % K
            w, row = (W_hn if bool(q) != bottom else W_on), bottom * D + k * P
        else:
            w, row = W_1, (c - C_L1) * P
        return w[row:row + P, :]

    with ExitStack() as ctx:
        place = [(nc.sbuf_base + 31) // 32 * 32]
        size = {F32: 4, F32R: 4, I32: 4, BF16: 2, F16: 2}

        def sb(name, shape, dt, over=None):
            n = size[dt]
            for d in shape[1:]:
                n *= d
            at = place[0] if over is None else over
            t = nc.alloc_sbuf_tensor_at(name, shape, dt, offset=at)
            if over is None:
                place[0] += (n + 31) // 32 * 32
                assert place[0] <= nc.sbuf_usable_end, (name, place[0])
            return t, at

        def sem(name):
            return ctx.enter_context(nc.semaphore(name))

        banks = ctx.enter_context(nc.psum_tensor("banks", [P, 8 * H], F32))
        bank = [banks[:, i * H:(i + 1) * H] for i in range(8)]

        xf, _ = sb("xf", [P, B, D], F32)
        fT_hi, _ = sb("fT_hi", [P, K, N], F32R)
        fT_lo, _ = sb("fT_lo", [P, K, N], F32R)
        w_raw, _ = sb("w_raw", [P, 2, D], F32)
        w_hi, at = sb("w_hi", [P, 4, D], F32R)
        w_lo, _ = sb("w_lo", [P, 4, D], F32R)
        RING = 4
        pair_size = 2 * (3 + 1) * N * 2
        pick_dst = [sb(f"pick_dst{r}", [P, 2, 3, N], BF16, over=at + r * pair_size)[0] for r in range(RING)]
        pick_src = [sb(f"pick_src{r}", [P, 2, N], BF16, over=at + r * pair_size + 2 * 3 * N * 2)[0]
                    for r in range(RING)]
        member, at = sb("member", [P, B, E], BF16)
        hn_hi, _ = sb("hn_hi", [P, B, D], F32R, over=at)
        hn_lo, _ = sb("hn_lo", [P, B, D], F32R, over=at + B * D * 4)
        hf, _ = sb("hf", [P, B, D], F32, over=at + 2 * B * D * 4)
        adjwT, _ = sb("adjwT", [P, B, N], F32, over=at + 3 * B * D * 4)
        ROWS = 6
        rows, at = sb("rows", [P, ROWS, D], F32)
        dst_rep, _ = sb("dst_rep", [P, ROWS, CE], I32, over=at)
        adjT_hi, _ = sb("adjT_hi", [P, B, N], F32R, over=at)
        adjT_lo, _ = sb("adjT_lo", [P, B, N], F32R, over=at + B * N * 4)
        stage, at = sb("stage", [P, 4, H], F32)
        h_edge, _ = sb("h_edge", [P, TILE_HH, D], F32, over=at)
        adj, _ = sb("adj", [P, B, N], F32, over=at)
        wa_rep, _ = sb("wa_rep", [P, D], F32)
        bias, at = sb("bias", [P, 2, D], F32)
        masked, _ = sb("masked", [P, CE], BF16, over=at + D * 4)
        lift, at = sb("lift", [P, CE], F32)
        ids_row, _ = sb("ids_row", [T, 2, P], I32, over=at)
        ids_rowf, _ = sb("ids_rowf", [T, 3, P], F32, over=at + 2 * P * 4)
        e_part, at = sb("e_part", [P, 3, T], F32)
        pair_row, _ = sb("pair_row", [1, 3, T // 2], F32, over=at)
        nibble, _ = sb("nibble", [1, T // 8, 4], F32, over=at + 3 * T // 2 * 4)
        ident, _ = sb("ident", [P, P], F32)
        node_no, _ = sb("node_no", [P, N], F16)
        zeros, _ = sb("zeros", [P, P], BF16)
        ids_f, _ = sb("ids_f", [P, 3, T], F32)
        ids_i, _ = sb("ids_i", [P, 2, T], I32)
        node_id, _ = sb("node_id", [P, B], F32)
        w_part, _ = sb("w_part", [P, 3, T], F32)
        pair_end, _ = sb("pair_end", [P, T], BF16)
        tile_lo, _ = sb("tile_lo", [T, 2], F32)
        pair_word, _ = sb("pair_word", [1, T // 8], I32)
        w_col, at = sb("w_col", [P, T, 4], BF16)
        part16, _ = sb("part16", [P, T], BF16)
        rest, _ = sb("rest", [P, T], F32, over=at)
        at_w_col = at
        logit, at = sb("logit", [P, T], F32)
        ex, _ = sb("ex", [P, T], F32, over=at)
        lb, _ = sb("lb", [P, T], F32)
        lifted, _ = sb("lifted", [P, 2, 32], F32)
        liftT, _ = sb("liftT", [P, 2, 32], F32)
        me, _ = sb("me", [P, T], F32, over=at_w_col + T * 4)
        ba_rep, _ = sb("ba_rep", [P, 1], F32)
        ones_f, _ = sb("ones_f", [P, 1], F32)
        nhalf, _ = sb("nhalf", [P, B], F32)
        stats, _ = sb("stats", [P, B, 2, 6], F32)
        mv, _ = sb("mv", [P, B, 2], F32)
        veps, _ = sb("veps", [P, B], F32)
        rstd, _ = sb("rstd", [P, B], F32)
        count, _ = sb("count", [P, B, NC], F32)
        cmax, _ = sb("cmax", [P, B, NC], F32)
        deg_in, _ = sb("deg_in", [P, B], F32)
        deg_out, _ = sb("deg_out", [P, B], F32)
        wsum, _ = sb("wsum", [P, B], F32)
        w_out, _ = sb("w_out", [P, B], F32)
        f_dst, _ = sb("f_dst", [P, B], F32)
        f_src, _ = sb("f_src", [P, B], F32)
        rden, _ = sb("rden", [P, B], F32)
        mx, _ = sb("mx", [P, B], F32)
        mrest, _ = sb("mrest", [P, B], F32)
        mpart, _ = sb("mpart", [P, B, 3], BF16)

        table = [[nc.dram_tensor(f"table{k}{s}", [N, D], F32, kind="Internal").ap() for s in range(2)]
                 for k in range(len(kinds))]
        h_row = nc.dram_tensor("h_row", [N, D], F32, kind="Internal").ap()
        lift_row = nc.dram_tensor("lift_row", [NC, CT, P], F32, kind="Internal").ap()

        h_out = sem("h_out"); h_back = sem("h_back")
        hh_in = [sem(f"hh_in{r}") for r in range(TILE_HH)]
        hhT_ready = sem("hhT_ready"); hh_hi_done = sem("hh_hi_done"); hh_lo_done = sem("hh_lo_done")
        hh_logits = sem("hh_logits")
        words_ready = sem("words_ready"); x_in = [sem(f"x_in{b}") for b in range(B)]
        ids_in = sem("ids_in"); wa_in = sem("wa_in")
        dst_in = [sem(f"dst_in{s}") for s in range(ROWS)]
        bias_in = [sem(f"bias_in{s}") for s in range(2)]
        w_in = [sem(f"w_in{s}") for s in range(2)]
        stored = [sem(f"stored{s}") for s in range(4)]
        row_in = [sem(f"row_in{s}") for s in range(ROWS)]
        hi_done = sem("hi_done"); lo_done = sem("lo_done"); chunk_used = sem("chunk_used")
        bank_done = sem("bank_done"); evac = sem("evac")
        consts = sem("consts"); own = sem("dve_step"); pool_step = sem("pool_step")
        idsf_ready = sem("idsf_ready"); idsT_ready = sem("idsT_ready"); ids_ready = sem("ids_ready")
        var_ready = sem("var_ready"); rstd_ready = sem("rstd_ready")
        h_pre = sem("h_pre"); h_ready = sem("h_ready"); hT_ready = sem("hT_ready")
        fT_hi_done = sem("fT_hi_done"); fT_lo_done = sem("fT_lo_done")
        member_done = sem("member_done"); edge_done = sem("edge_done")
        lift_ready = sem("lift_ready"); lift_out = sem("lift_out"); lift_in = sem("lift_in"); max_done = sem("max_done")
        dst_picked = sem("dst_picked"); src_picked = sem("src_picked"); src0_picked = sem("src0_picked")
        own_act = sem("act_step"); adj_done = sem("adj_done"); adj_full = sem("adj_full")
        adj_ready = sem("adj_ready"); adjT_done = sem("adjT_done"); adjwT_ready = sem("adjwT_ready")
        wsum_ready = sem("wsum_ready"); wdeg_ready = sem("wdeg_ready"); fac_ready = sem("fac_ready")
        mpart_ready = sem("mpart_ready"); me_done = sem("me_done"); arg_ready = sem("arg_ready"); ex_ready = sem("ex_ready")
        adjT_hi_done = sem("adjT_hi_done"); adjT_lo_done = sem("adjT_lo_done")
        hn_hi_done = sem("hn_hi_done"); hn_lo_done = sem("hn_lo_done")
        z_done = sem("z_done"); x_again = sem("x_again")
        x2_step = sem("x2_step"); out_ready = sem("out_ready")
        out_stored = [sem(f"out_stored{s}") for s in range(4)]

        TOP, HH, BOT, L1 = UNITS, UNITS + 1, UNITS + 2, UNITS + 3
        first_chunk = {TOP: C_TOP, HH: C_HH, BOT: C_BOT, L1: C_L1}
        done_before = {TOP: 7 * UNITS, HH: 7 * UNITS + 6, BOT: 7 * UNITS + 9, L1: 7 * UNITS + 15}

        def bank_ready(eng, unit, j):
            first, before = first_chunk.get(unit, K * unit), done_before.get(unit, 7 * unit)
            if unit == BOT:
                if j in (1, 7):
                    eng.wait_ge(chunk_used, first + (K if j == 1 else 2 * K))
                else:
                    eng.wait_ge(bank_done, before + max(j, 1))
            elif unit == TOP:
                if j in (1, 7):
                    eng.wait_ge(chunk_used, first + (2 * K if j == 1 else K))
                else:
                    eng.wait_ge(bank_done, before + (j - 1 if j > 1 else 6))
            elif j == (3 if unit == HH else 7):
                eng.wait_ge(chunk_used, first + (2 * K if unit == HH else K))
            else:
                eng.wait_ge(bank_done, before + j + 1)

        MIX = 34

        def pairs_after(i):
            return range(i, i + 1) if i < TE - MIX - 1 else range(i, T // 2)

        def send_lift(eng, c):
            eng.wait_ge(lift_ready, c + 1)
            for a in range(0, P, 32):
                eng.dma_start(lift_row[c, :, a:a + 32], liftT[a:a + CT, c % 2, :]).then_inc(lift_out, 16)

        def fetch_lift(eng, c):
            eng.wait_ge(lift_out, 16 * 4 * (c + 1))
            if c >= 1:
                eng.wait_ge(max_done, B * c)
            eng.dma_start(lift[:, :], lift_row[c].rearrange("t p -> (t p)").partition_broadcast(P)).then_inc(lift_in, 16)

        block = ctx.enter_context(nc.Block())
        AB = ((0, 0), (0, 1), (1, 0))
        fT, wS, hn, adjT = (fT_hi, fT_lo), (w_hi, w_lo), (hn_hi, hn_lo), (adjT_hi, adjT_lo)

        @block.sync
        def _(sp):
            for b in range(B):
                sp.dma_start(xf[:, b, :], x[b * P:(b + 1) * P, :]).then_inc(x_in[b], 16)
            for a, arr in enumerate((src, dst, edge_w)):
                tgt = ids_row[:, a, :] if a < 2 else ids_rowf[:, a, :]
                for i0, t0, n in RUNS:
                    sp.dma_start(tgt[i0:i0 + n], arr[t0 * P:(t0 + n) * P].rearrange("(t p) -> t p", p=P)).then_inc(ids_in, 16)

            def load(c):
                if c >= 2:
                    sp.wait_ge(lo_done, c - 1)
                sp.dma_start(w_raw[:, c % 2, :], chunk_rows(c)).then_inc(w_in[c % 2], 16)

            def load_bias(n, vec):
                sp.dma_start(bias[:, n % 2, :], vec.partition_broadcast(P)).then_inc(bias_in[n % 2], 16)

            load(0)
            load(1)
            sp.dma_start(wa_rep[:, :], W_a.rearrange("d o -> (d o)").partition_broadcast(P)).then_inc(wa_in, 16)
            sp.dma_start(ba_rep[:, :], b_a.partition_broadcast(P)).then_inc(wa_in, 16)
            load_bias(0, b_ho)
            load_bias(1, b_oo)
            for c in range(2, K + 6):
                if c == K:
                    sp.wait_ge(h_ready, B)
                    sp.dma_start(h_row.rearrange("(b p) d -> p b d", p=P), xf[:, :, :]).then_inc(h_out, 16)
                load(c)
            for u in range(UNITS):
                for j in range(8):
                    e = 8 * u + j
                    sp.wait_ge(evac, e + 1)
                    m, n = j // 2, j % 2
                    sp.dma_start(table[u // 2][u % 2][m * P:(m + 1) * P, n * H:(n + 1) * H],
                                 stage[:, e % 4, :]).then_inc(stored[e % 4], 16)
                if u % 2 == 1:
                    load_bias(2 + u // 2, (b_hn, b_on)[u // 2])
                for c in range(K * (u + 1) + 6, K * (u + 2) + 6):
                    load(c)
            for c in range(C_TOP + 6 + K, C_HH + 6):
                load(c)
            sp.wait_ge(evac, 8 * UNITS + 8)
            load_bias(4, b_hh)
            for c in range(C_HH + 6, C_BOT + 2):
                load(c)
            fetch_lift(sp, 3)
            for c in range(4, NC):
                send_lift(sp, c)
                fetch_lift(sp, c)
            sp.wait_ge(me_done, 1)
            load_bias(5, b_1)
            sp.dma_start(hf[:, :, :], h_row.rearrange("(b p) d -> p b d", p=P)).then_inc(h_back, 16)
            sp.wait_ge(hn_lo_done, B)
            for c in range(C_BOT + 2, C_BOT + 6):
                load(c)
            for b in range(B):
                sp.dma_start(hf[:, b, :], x[b * P:(b + 1) * P, :]).then_inc(x_again, 16)
            for c in range(C_BOT + 6, C_END):
                load(c)
            for j in range(8):
                m, n = j // 2, j % 2
                sp.wait_ge(out_ready, j + 1)
                sp.dma_start(out[m * P:(m + 1) * P, n * H:(n + 1) * H], stage[:, j % 4, :]).then_inc(out_stored[j % 4], 16)
            for s in range(4):
                sp.wait_ge(out_stored[s], 32)

        @block.gpsimd
        def _(pool):
            pool.memset(ident[:, :], 0.0).then_inc(pool_step, 1)
            pool.iota(node_no[:, :], [[1, N]], base=0, channel_multiplier=0,
                      allow_small_or_imprecise_dtypes=True).then_inc(consts, 1)
            pool.iota(node_id[:, :], [[P, B]], base=0, channel_multiplier=1,
                      allow_small_or_imprecise_dtypes=True).then_inc(consts, 1)
            pool.memset(ones_f[:, :], 1.0).then_inc(consts, 1)
            pool.memset(zeros[:, :], 0.0).then_inc(consts, 1)
            pool.memset(nhalf[:, :], -0.5).then_inc(consts, 1)
            pool.wait_ge(pool_step, 1)
            pool.affine_select(out=ident[:, :], in_=ident[:, :], compare_op=ALU.not_equal, fill=1.0, base=0,
                               pattern=[[-1, P]], channel_multiplier=1).then_inc(consts, 1)
            pool.wait_ge(consts, 6)

            def power(n, dst_t, src_t, ready, done):
                pool.wait_ge(ready, n)
                pool.tensor_tensor(dst_t[:, :], src_t[:, :], nhalf[:, :], ALU.pow).then_inc(done, 1)

            power(1, rstd, veps, var_ready, rstd_ready)
            pool.wait_ge(ids_ready, 1)

            def fetch_src(i, kind, s, lap):
                pool.indirect_dma_start(out=rows[:, s, :], out_offset=None, in_=table[kind][0],
                                        in_offset=bass.IndirectOffsetOnAxis(ap=ids_i[:, 0, i:i + 1], axis=0)
                                        ).then_inc(row_in[s], 16)

            def add_dst(i, kind, s, lap):
                pool.wait_ge(row_in[s], lap * 32 + 16)
                pool.indirect_dma_start(out=rows[:, s, :], out_offset=None, in_=table[kind][1],
                                        in_offset=bass.IndirectOffsetOnAxis(ap=ids_i[:, 1, i:i + 1], axis=0),
                                        compute_op=ALU.add).then_inc(row_in[s], 16)

            def tables_stored(kind):
                for s in range(4):
                    pool.wait_ge(stored[s], 16 * 4 * (kind + 1))

            tables_stored(0)
            AHEAD = 3

            def step(i):
                j = i + AHEAD
                if j < TE:
                    if kind_of(j) != kind_of(j - 1):
                        tables_stored(kind_of(j))
                    if j >= ROWS:
                        pool.wait_ge(edge_done, j - ROWS + 1)
                    fetch_src(j, kind_of(j), j % ROWS, j // ROWS)
                add_dst(i, kind_of(i), i % ROWS, i // ROWS)

            for i in range(AHEAD):
                fetch_src(i, 0, i, 0)
            def fetch_h(side):
                for r in range(TILE_HH):
                    i = TE + r
                    pool.indirect_dma_start(out=h_edge[:, r, :], out_offset=None, in_=h_row,
                                            in_offset=bass.IndirectOffsetOnAxis(ap=ids_i[:, side, i:i + 1], axis=0)
                                            ).then_inc(hh_in[r], 16)

            for i in range(TE):
                if i == 22:
                    for s in range(4):
                        pool.wait_ge(stored[s], 2 * 16 * UNITS)
                    pool.wait_ge(h_out, 16)
                    fetch_h(0)
                if i == 29:
                    pool.wait_ge(hhT_ready, K // 2)
                    fetch_h(1)
                step(i)
            power(1, f_dst, wsum, wsum_ready, fac_ready)
            power(1, f_src, w_out, wdeg_ready, fac_ready)
            for pair in range(T // 2):
                pool.wait_ge(adj_done, T // 2 + pair - (RING - 1))
                t = 2 * pair
                pool.tensor_scalar(pick_src[pair % RING][:, 0, :], node_no[:, :], ids_f[:, 0, t:t + 1], None,
                                   ALU.is_equal).then_inc(src0_picked, 1)
            for n in range(B):
                power(2 + n, rstd, veps, var_ready, rstd_ready)

        @block.scalar
        def _(act):
            def dst_rep_load(c):
                i0 = c * CT
                for p0, t0, n in RUNS:
                    a, z = max(i0, p0), min(i0 + CT, p0 + n)
                    if a < z:
                        t = t0 + a - p0
                        act.dma_start(dst_rep[:, c % ROWS, (a - i0) * P:(z - i0) * P],
                                      dst[t * P:(t + z - a) * P].partition_broadcast(P)).then_inc(dst_in[c % ROWS], 16)

            def hi(c):
                act.wait_ge(w_in[c % 2], 16 * (c // 2 + 1))
                act.activation(w_hi[:, c, :], w_raw[:, c % 2, :], ACT.Copy).then_inc(hi_done, 1)

            hi(0)
            for b in range(B):
                act.wait_ge(h_pre, b + 1)
                act.activation(xf[:, b, :], xf[:, b, :], ACT.Relu).then_inc(h_ready, 1)
            hi(1)
            for f in range(K):
                act.wait_ge(hT_ready, f + 1)
                act.activation(fT_hi[:, f, :], bank[f][:, :], ACT.Copy).then_inc(fT_hi_done, 1)
            hi(2)
            for c in range(ROWS):
                dst_rep_load(c)
            hi(3)

            def hi_quad(c0, lap):
                for r in range(4):
                    act.wait_ge(w_in[r % 2], lap * 32 + 16 * (r // 2 + 1))
                    act.wait_ge(chunk_used, c0 + (r - 3))
                    act.activation(w_hi[:, r, :], w_raw[:, r % 2, :], ACT.Copy).then_inc(hi_done, 1)

            def evacuate(u):
                for j in range(8):
                    e = 8 * u + j
                    bank_ready(act, u, j)
                    if e >= 4:
                        act.wait_ge(stored[e % 4], 16 * (e // 4))
                    act.activation(stage[:, e % 4, :], bank[j][:, :], ACT.Copy).then_inc(evac, 1)

            for u in range(UNITS):
                with act.Fori(2 * u + 1, 2 * u + 3) as q:
                    hi_quad(q * 4, q)
                if u == 0:
                    for c in range(ROWS, NC):
                        act.wait_ge(member_done, c - ROWS + 1)
                        dst_rep_load(c)
                if u % 2 == 0:
                    evacuate(u)
            send_lift(act, 0)
            with act.Fori(2 * UNITS + 1, 2 * UNITS + 3) as q:
                hi_quad(q * 4, q)
            fetch_lift(act, 0)
            send_lift(act, 1)
            hi_quad(C_HH - 4, C_HH // 4 - 1)

            def high_of_edges(side):
                for g in range(K // 2):
                    act.wait_ge(hhT_ready, side * (K // 2) + g + 1)
                    act.activation(fT_hi[:, 2 * g:2 * g + 2, side * 2 * P:(side + 1) * 2 * P],
                                   bank[4 + g].rearrange("p (f e) -> p f e", f=2), ACT.Copy).then_inc(hh_hi_done, 1)

            hi_quad(C_HH, C_HH // 4)
            act.wait_ge(chunk_used, C_HH)
            high_of_edges(0)
            hi_quad(C_HH + 4, C_HH // 4 + 1)
            high_of_edges(1)
            fetch_lift(act, 1)
            send_lift(act, 2)
            with act.Fori(C_HH // 4 + 2, C_HH // 4 + 4) as q:
                hi_quad(q * 4, q)
            fetch_lift(act, 2)
            send_lift(act, 3)
            mine = [0]

            def pick(pair, tiles, first_pair):
                slot = pair % RING
                if first_pair + pair >= RING:
                    act.wait_ge(adj_done, first_pair + pair - (RING - 1))
                for r in tiles:
                    t = pair * 2 + r
                    act.activation(pick_src[slot][:, r, :].bitcast(F16), node_no[:, :], ACT.Abs, bias=ids_f[:, 0, t:t + 1],
                                   scale=-1.0).then_inc(own_act, 1)
                    mine[0] += 1
                act.wait_ge(own_act, mine[0])
                part = pick_src[slot][:, tiles[0]:2, :]
                act.activation(part, part.bitcast(F16), ACT.Relu, bias=ones_f[:, 0:1], scale=-1.0).then_inc(src_picked, 1)

            for pair in range(T // 2):
                if pair == 0:
                    act.wait_ge(hh_logits, TILE_HH)
                pick(pair, (0, 1), 0)
            EARLY = 3
            for pair in range(EARLY):
                pick(pair, (1,), T // 2)
            act.wait_ge(arg_ready, 1)
            act.activation(ex[:, :], me[:, :], ACT.Exp, scale=-1.0).then_inc(ex_ready, 1)
            for s in range(B):
                act.wait_ge(adjT_done, s + 1)
                act.activation(adjwT[:, s, :], bank[4 + s][:, :], ACT.Copy).then_inc(adjwT_ready, 1)
            for pair in range(EARLY, T // 2):
                pick(pair, (1,), T // 2)
                if pair % CT == CT - 1:
                    act.wait_ge(h_back, 16)
                    b = pair // CT
                    act.activation(hn_hi[:, b, :], hf[:, b, :], ACT.Copy).then_inc(hn_hi_done, 1)
            for s in range(B):
                act.wait_ge(adjT_done, B + s + 1)
                act.activation(adjT_hi[:, s, :], bank[4 + s][:, :], ACT.Copy).then_inc(adjT_hi_done, 1)
            hi_quad(C_BOT, C_BOT // 4)
            for f in range(K):
                act.wait_ge(z_done, f + 1)
                act.activation(fT_hi[:, f, :], bank[f][:, :], ACT.Copy).then_inc(fT_hi_done, 1)
            act.wait_ge(adjwT_ready, B)
            for s in range(B):
                act.activation(adjT_hi[:, s, :], adjwT[:, s, :], ACT.Copy).then_inc(adjT_hi_done, 1)
            with act.Fori(C_BOT // 4 + 1, C_L1 // 4) as q:
                hi_quad(q * 4, q)
            for b in range(B):
                act.wait_ge(h_pre, B + b + 1)
                act.activation(hn_hi[:, b, :], hf[:, b, :], ACT.Relu).then_inc(hn_hi_done, 1)
            hi_quad(C_L1, C_L1 // 4)
            for f in range(K):
                act.wait_ge(z_done, K + f + 1)
                act.activation(fT_hi[:, f, :], bank[f][:, :], ACT.Copy).then_inc(fT_hi_done, 1)
            hi_quad(C_L1 + 4, C_L1 // 4 + 1)

        @block.vector
        def _(dve):
            step = Step(dve, own)

            def build_member(c, b):
                if b == 0:
                    dve.wait_ge(dst_in[c % ROWS], 16 * dst_loads(c))
                ins = dve.tensor_scalar(member[:, b, c * CE:(c + 1) * CE], dst_rep[:, c % ROWS, :],
                                        node_id[:, b:b + 1], 0.0, ALU.is_equal, ALU.add, accum_out=count[:, b, c:c + 1])
                if b == B - 1:
                    ins.then_inc(member_done, 1)

            def dst_loads(c):
                total = 0
                for cc in range(c % ROWS, c + 1, ROWS):
                    for p0, t0, n in RUNS:
                        total += max(cc * CT, p0) < min(cc * CT + CT, p0 + n)
                return total

            def norm_stats(blocks, arrived=None):
                for b in blocks:
                    if arrived is not None:
                        dve.wait_ge(arrived[b], 16)
                    for n in range(2):
                        ins = dve.bn_stats(stats[:, b, n, :], xf[:, b, n * H:(n + 1) * H])
                    step(ins)
                    ins = dve.bn_aggr(mv[:, b, :], stats[:, b, :, :])
                    step(ins)

            def lo(c0, r, pe_free):
                dve.wait_ge(hi_done, c0 + (r + 1))
                if pe_free:
                    dve.wait_ge(chunk_used, c0 + (r - 3))
                dve.tensor_tensor(w_lo[:, r, :], w_raw[:, r % 2, :], w_hi[:, r, :].bitcast(F32), ALU.subtract
                                  ).then_inc(lo_done, 1)

            norm_stats(range(B), x_in)
            dve.tensor_scalar(veps[:, :], mv[:, :, 1], EPS, None, ALU.add).then_inc(var_ready, 1)
            lo(0, 0, False)
            dve.wait_ge(rstd_ready, 1)
            for b in range(B):
                dve.tensor_scalar(xf[:, b, :], xf[:, b, :], mv[:, b, 0:1], rstd[:, b:b + 1], ALU.subtract,
                                  ALU.mult).then_inc(h_pre, 1)
            dve.wait_ge(ids_in, 16 * 3 * len(RUNS))
            step(dve.tensor_copy(ids_rowf[:, 0:2, :], ids_row[:, 0:2, :]))
            dve.wait_ge(consts, 6)
            block_no = ids_row[:, 0, :].bitcast(F32)
            step(dve.tensor_scalar(block_no, ids_rowf[:, 1, :], float(P), None, ALU.is_ge))
            for b in range(2, B):
                step(dve.scalar_tensor_tensor(block_no, ids_rowf[:, 1, :], float(b * P), block_no, ALU.is_ge, ALU.add))
            dve.tensor_reduce(tile_lo[:, 0:1], block_no, AX.X, ALU.min)
            dve.tensor_reduce(tile_lo[:, 1:2], block_no, AX.X, ALU.max).then_inc(idsf_ready, 1)
            dve.wait_ge(idsT_ready, 1)
            step(dve.tensor_copy(ids_f[:, :, :], bank[K - 1][:, 0:3 * T].rearrange("p (a t) -> p a t", a=3)))
            dve.tensor_copy(ids_i[:, :, :], ids_f[:, 0:2, :]).then_inc(ids_ready, 1)
            for k, op in enumerate((ALU.min, ALU.max)):
                step(dve.tensor_reduce(pair_row[:, k, :], bank[K - 1][0:1, (3 + k) * T:(4 + k) * T].rearrange(
                    "o (p r) -> o p r", r=2), AX.X, op))
            for k in range(4):
                ins = dve.memset(nibble[:, :, k:k + 1], float(16 ** k))
            step(ins)
            step(dve.scalar_tensor_tensor(pair_row[:, 2, :], pair_row[:, 1, :], 4.0, pair_row[:, 0, :], ALU.mult, ALU.add))
            step(dve.tensor_tensor(nibble[:, :, :], nibble[:, :, :], pair_row[:, 2, :].rearrange("o (w k) -> o w k", k=4),
                                   ALU.mult))
            step(dve.tensor_reduce(pair_row[:, 0, 0:T // 8], nibble[:, :, :], AX.X, ALU.add))
            dve.tensor_copy(pair_word[:, :], pair_row[:, 0, 0:T // 8]).then_inc(words_ready, 1)

            def split3(parts, whole, n):
                src_ap = whole
                for k in range(3):
                    step(dve.tensor_copy(part16[:, :], src_ap))
                    step(dve.tensor_copy(parts[:, k, :], part16[:, :]))
                    if k < 2:
                        step(dve.tensor_tensor(rest[:, :], src_ap, parts[:, k, :], ALU.subtract))
                        src_ap = rest[:, :]

            for f in range(K):
                dve.wait_ge(fT_hi_done, f + 1)
                dve.tensor_tensor(fT_lo[:, f, :], bank[f][:, :], fT_hi[:, f, :].bitcast(F32), ALU.subtract
                                  ).then_inc(fT_lo_done, 1)

            def edge(i):
                r = i % ROWS
                dve.wait_ge(row_in[r], i // ROWS * 32 + 32)
                dve.scalar_tensor_tensor(rows[:, r, :], rows[:, r, :], 0.0, wa_rep[:, :], ALU.max, ALU.mult,
                                         accum_out=logit[:, i:i + 1]).then_inc(edge_done, 1)

            def lift_chunk(c):
                a, z = c * CT, (c + 1) * CT
                dve.wait_ge(edge_done, min(z, TE))
                if c == NC - 1:
                    dve.wait_ge(hh_logits, TILE_HH)
                step(dve.tensor_scalar(lb[:, a:z], logit[:, a:z], ba_rep[:, 0:1], None, ALU.add))
                step(dve.tensor_scalar(lifted[:, c % 2, 0:CT], lb[:, a:z], BIG, None, ALU.add))
                if c >= 2:
                    dve.wait_ge(lift_out, 16 * 4 * (c - 1))
                dve.transpose(liftT[:, c % 2, :], lifted[:, c % 2, :]).then_inc(lift_ready, 1)

            def chunk_max(c):
                dve.wait_ge(lift_in, 16 * (c + 1))
                for b in range(B):
                    if c or b:
                        dve.wait_ge(max_done, B * c + b)
                    dve.tensor_tensor_reduce(masked[:, :], lift[:, :], member[:, b, c * CE:(c + 1) * CE], 1.0, 0.0,
                                             ALU.mult, ALU.max, cmax[:, b, c:c + 1]).then_inc(max_done, 1)

            def evacuate(u):
                kind = u // 2
                dve.wait_ge(bias_in[kind % 2], 16 * (kind // 2 + 1))
                for j in range(8):
                    e = 8 * u + j
                    bank_ready(dve, u, j)
                    dve.wait_ge(stored[e % 4], 16 * (e // 4))
                    n = j % 2
                    dve.tensor_tensor(stage[:, e % 4, :], bank[j][:, :], bias[:, kind % 2, n * H:(n + 1) * H],
                                      ALU.add).then_inc(evac, 1)

            for r in range(1, 4):
                lo(0, r, False)
            split3(w_part, ids_f[:, 2, :], T)
            dve.memset(w_col[:, :, 0:1], 1.0)
            step(dve.tensor_copy(w_col[:, :, 1:4], w_part.rearrange("p k t -> p t k")))
            step(dve.memset(lifted[:, :, :], 0.0))
            dve.wait_ge(words_ready, 1)
            dve.wait_ge(wa_in, 32)
            for u in range(UNITS + 1):
                if u < 2:
                    for c in range(8 * u + 4, 8 * u + 12):
                        lo(c // 4 * 4, c % 4, True)
                        for part in (2 * (c - 4), 2 * (c - 4) + 1):
                            build_member(part // B, part % B)
                else:
                    for c in range(8 * u + 4, 8 * u + 12):
                        lo(c // 4 * 4, c % 4, True)
                        edge(c - 8 * u - 4 + 8 * (u - 2))
                if u < UNITS and u % 2 == 1:
                    evacuate(u)
                if u == 1:
                    dve.wait_ge(member_done, NC)
                    step(dve.tensor_reduce(deg_in[:, :], count[:, :, :], AX.X, ALU.add))
                if u >= 2:
                    lift_chunk(u - 2)
            at_edge = 8 * (UNITS - 1)

            dve.wait_ge(bias_in[1], 32)
            dve.wait_ge(bias_in[0], 32)
            dve.wait_ge(h_out, 16)

            def keep_top(banks):
                for j in banks:
                    m, n = j // 2, j % 2
                    bank_ready(dve, TOP, j)
                    dve.tensor_tensor(xf[:, m, n * H:(n + 1) * H], bank[j][:, :],
                                      bias[:, 0 if m < BLOCK_H else 1, n * H:(n + 1) * H], ALU.add).then_inc(evac, 1)

            def low_of_edges(side):
                for g in range(K // 2):
                    dve.wait_ge(hh_hi_done, side * (K // 2) + g + 1)
                    part = (slice(None), slice(2 * g, 2 * g + 2), slice(side * 2 * P, (side + 1) * 2 * P))
                    dve.tensor_tensor(fT_lo[part], bank[4 + g].rearrange("p (f e) -> p f e", f=2),
                                      fT_hi[part].bitcast(F32), ALU.subtract).then_inc(hh_lo_done, 1)

            def lo_and_edges(c0, i):
                for r in range(4):
                    lo(c0, r, True)
                    if r % 2 == 1:
                        edge(i + r // 2)

            keep_top(range(2, 8))
            lo_and_edges(C_HH - 4, at_edge)
            for r in range(4):
                lo(C_HH, r, True)
            keep_top(range(2))
            low_of_edges(0)
            chunk_max(0)
            edge(at_edge + 2)
            edge(at_edge + 3)
            lo_and_edges(C_HH + 4, at_edge + 4)
            low_of_edges(1)
            lo_and_edges(C_HH + 8, at_edge + 6)
            lift_chunk(3)
            chunk_max(1)
            lo_and_edges(C_HH + 12, at_edge + 8)
            dve.wait_ge(bias_in[0], 48)
            for r in range(TILE_HH):
                for n in range(2):
                    bank_ready(dve, HH, 2 * r + n)
                    ins = dve.tensor_tensor(h_edge[:, r, n * H:(n + 1) * H], bank[2 * r + n][:, :],
                                            bias[:, 0, n * H:(n + 1) * H], ALU.add)
                step(ins)
                dve.scalar_tensor_tensor(h_edge[:, r, :], h_edge[:, r, :], 0.0, wa_rep[:, :], ALU.max, ALU.mult,
                                         accum_out=logit[:, TE + r:TE + r + 1]).then_inc(hh_logits, 1)

            def spread(word, pair, parts, first_pair):
                k, slot = pair % 4, pair % RING
                if first_pair + pair >= RING:
                    dve.wait_ge(adj_done, first_pair + pair - (RING - 1))
                lo_b, hi_b = dve.snap((word >> (4 * k)) & 3), dve.snap((word >> (4 * k + 2)) & 3)
                with dve.Fori(lo_b, hi_b + 1) as b:
                    for r in range(2):
                        t = pair * 2 + r
                        dve.scalar_tensor_tensor(pick_dst[slot][:, r, :, bass.ds(b * P, P)],
                                                 node_no[:, None, bass.ds(b * P, P)].broadcast_to([P, 3, P]),
                                                 ids_f[:, 1, t:t + 1], parts[:, :, t:t + 1].broadcast_to([P, 3, P]),
                                                 ALU.is_equal, ALU.mult)
                dve.memset(pair_end[:, first_pair + pair:first_pair + pair + 1], 0.0).then_inc(dst_picked, 1)

            words = [dve.value_load(pair_word[0:1, q:q + 1], min_val=0, max_val=16 ** 4 - 1) for q in range(T // 8)]

            for t in range(MIX, TE):
                edge(t)
                if t % CT == CT - 1 or t == TE - 1:
                    lift_chunk(t // CT)
                for pair in pairs_after(t - MIX):
                    spread(words[pair // 4], pair, w_part, 0)
                if t in (MIX + 1, MIX + 4):
                    chunk_max(2 + (t - MIX) // 4)
                elif t > MIX + 4 and t % CT == 3:
                    chunk_max((t - CT) // CT)
            chunk_max(7)
            dve.wait_ge(max_done, B * NC)
            step(dve.tensor_reduce(mx[:, :], cmax[:, :, :], AX.X, ALU.max))
            left = mx
            for k in range(3):
                ins = dve.tensor_copy(mpart[:, :, k], left[:, :])
                if k == 2:
                    ins.then_inc(mpart_ready, 1)
                else:
                    step(ins)
                    step(dve.tensor_tensor(mrest[:, :], left[:, :], mpart[:, :, k], ALU.subtract))
                    left = mrest
            dve.wait_ge(adj_full, 1)
            for b in range(B):
                ins = dve.tensor_reduce(wsum[:, b:b + 1], bank[b][:, :], AX.X, ALU.add)
            step(ins)
            step(dve.tensor_scalar(wsum[:, :], wsum[:, :], TINY, None, ALU.max))
            step(dve.tensor_scalar(deg_in[:, :], deg_in[:, :], 1.0, None, ALU.max))
            step(dve.tensor_tensor(mrest[:, :], wsum[:, :], deg_in[:, :], ALU.mult))
            dve.tensor_copy(wsum[:, :], mrest[:, :]).then_inc(wsum_ready, 1)
            sums = bank[4][:, 0:4 * B].rearrange("p (b k) -> p b k", k=4)
            step(dve.tensor_scalar(deg_out[:, :], sums[:, :, 0], 1.0, None, ALU.max))
            step(dve.tensor_reduce(mrest[:, :], sums[:, :, 1:4], AX.X, ALU.add))
            step(dve.tensor_scalar(mrest[:, :], mrest[:, :], TINY, None, ALU.max))
            dve.tensor_tensor(w_out[:, :], mrest[:, :], deg_out[:, :], ALU.mult).then_inc(wdeg_ready, 1)
            dve.wait_ge(fac_ready, 1)
            for b in range(B):
                dve.tensor_scalar(adj[:, b, :], bank[b][:, :], f_dst[:, b:b + 1], None, ALU.mult).then_inc(adj_ready, 1)
            dve.wait_ge(me_done, 1)
            step(dve.tensor_reduce(me[:, :], bank[5][:, 0:3 * T].rearrange("p (t k) -> p t k", k=3), AX.X, ALU.add))
            step(dve.tensor_scalar(rest[:, :], me[:, :], -BIG, None, ALU.add))
            dve.tensor_tensor(me[:, :], rest[:, :], lb[:, :], ALU.subtract).then_inc(arg_ready, 1)
            dve.wait_ge(ex_ready, 1)
            split3(e_part, ex[:, :], T)
            for b in range(B):
                for q in range(2 * b, 2 * b + 2):
                    for k in range(4):
                        spread(words[q], q * 4 + k, e_part, T // 2)
                dve.wait_ge(hn_hi_done, b + 1)
                dve.tensor_tensor(hn_lo[:, b, :], hf[:, b, :], hn_hi[:, b, :].bitcast(F32), ALU.subtract
                                  ).then_inc(hn_lo_done, 1)
            dve.wait_ge(adj_full, 2)
            for b in range(B):
                ins = dve.tensor_reduce(wsum[:, b:b + 1], bank[b][:, :], AX.X, ALU.add)
            step(ins)
            step(dve.tensor_scalar(wsum[:, :], wsum[:, :], TINY, None, ALU.max))
            step(dve.reciprocal(rden[:, :], wsum[:, :]))
            for b in range(B):
                dve.tensor_scalar(adj[:, b, :], bank[b][:, :], rden[:, b:b + 1], None, ALU.mult).then_inc(adj_ready, 1)

            def low_of(dst_t, s, psum, hi_t, hi_sem, hi_n, done):
                dve.wait_ge(hi_sem, hi_n)
                dve.tensor_tensor(dst_t[:, s, :], psum, hi_t[:, s, :].bitcast(F32), ALU.subtract).then_inc(done, 1)

            for s in range(B):
                low_of(adjT_lo, s, bank[4 + s][:, :], adjT_hi, adjT_hi_done, s + 1, adjT_lo_done)
            for r in range(4):
                lo(C_BOT, r, True)
            for f in range(K):
                low_of(fT_lo, f, bank[f][:, :], fT_hi, fT_hi_done, K + f + 1, fT_lo_done)
            for s in range(B):
                low_of(adjT_lo, s, adjwT[:, s, :], adjT_hi, adjT_hi_done, B + s + 1, adjT_lo_done)
            with dve.Fori(C_BOT // 4 + 1, C_L1 // 4 - 1) as q:
                for r in range(4):
                    lo(q * 4, r, True)
            dve.wait_ge(x_again, 16 * B)
            dve.wait_ge(fac_ready, 2)

            def second_x(m):
                for n in range(2):
                    j, a, z = 2 * m + n, n * H, (n + 1) * H
                    bank_ready(dve, BOT, j)
                    step(dve.tensor_tensor(xf[:, m, a:z], bank[j][:, :], xf[:, m, a:z], ALU.add))
                    dve.scalar_tensor_tensor(xf[:, m, a:z], xf[:, m, a:z], 0.0, hf[:, m, a:z], ALU.max,
                                             ALU.add).then_inc(x2_step, 1)
                dve.wait_ge(x2_step, 2 * m + 2)
                norm_stats((m,))

            def root(m):
                dve.tensor_scalar(veps[:, :], mv[:, :, 1], EPS, None, ALU.add).then_inc(var_ready, 1)

            def second_h(m):
                dve.wait_ge(rstd_ready, 2 + m)
                step(dve.tensor_tensor(rstd[:, m:m + 1], rstd[:, m:m + 1], f_src[:, m:m + 1], ALU.mult))
                dve.tensor_scalar(hf[:, m, :], xf[:, m, :], mv[:, m, 0:1], rstd[:, m:m + 1], ALU.subtract,
                                  ALU.mult).then_inc(h_pre, 1)

            def second_h_lo(m):
                dve.wait_ge(hn_hi_done, B + m + 1)
                dve.scalar_tensor_tensor(hn_lo[:, m, :], hf[:, m, :], 0.0, hn_hi[:, m, :].bitcast(F32), ALU.max,
                                         ALU.subtract).then_inc(hn_lo_done, 1)

            second_x(0)
            root(0)
            for r in range(4):
                lo(C_L1 - 4, r, True)
            second_h(0)
            for m in range(1, B):
                second_x(m)
                root(m)
                second_h_lo(m - 1)
                second_h(m)
            second_h_lo(B - 1)
            for r in range(4):
                lo(C_L1, r, True)
            for f in range(K):
                low_of(fT_lo, f, bank[f][:, :], fT_hi, fT_hi_done, 2 * K + f + 1, fT_lo_done)
            for r in range(4):
                lo(C_L1 + 4, r, True)
            dve.wait_ge(bias_in[1], 48)
            for j in range(8):
                m, n = j // 2, j % 2
                a, z = n * H, (n + 1) * H
                bank_ready(dve, L1, j)
                if j >= 4:
                    dve.wait_ge(out_stored[j % 4], 16)
                step(dve.tensor_tensor(stage[:, j % 4, :], bank[j][:, :], bias[:, 1, a:z], ALU.add))
                dve.scalar_tensor_tensor(stage[:, j % 4, :], stage[:, j % 4, :], 0.0, xf[:, m, a:z], ALU.max,
                                         ALU.add).then_inc(out_ready, 1)

        @block.tensor
        def _(pe):
            pe.wait_ge(consts, 6)
            pe.wait_ge(idsf_ready, 1)
            for a in range(3):
                ins = pe.transpose(bank[K - 1][:, a * T:(a + 1) * T], ids_rowf[:, a, :], ident[0:T, 0:T])
            for k in range(2):
                ins = pe.transpose(bank[K - 1][0:1, (3 + k) * T:(4 + k) * T], tile_lo[:, k:k + 1], ident[0:T, 0:T])
            ins.then_inc(idsT_ready, 1)
            for b in range(B):
                pe.wait_ge(h_ready, b + 1)
                for f in range(K - 1):
                    ins = pe.transpose(bank[f][:, b * P:(b + 1) * P], xf[:, b, f * P:(f + 1) * P], ident[:, :])
                    if b == B - 1:
                        ins.then_inc(hT_ready, 1)
            pe.wait_ge(words_ready, 1)
            pe.wait_ge(ids_ready, 1)
            for b in range(B):
                ins = pe.transpose(bank[K - 1][:, b * P:(b + 1) * P], xf[:, b, (K - 1) * P:K * P], ident[:, :])
            ins.then_inc(hT_ready, 1)

            def chunk(c, k, slot, banks, evac_wait, first=False):
                pe.wait_ge(lo_done, c + 1)
                for j in banks:
                    if first and k == 0:
                        pe.wait_ge(fT_lo_done, j + 1)
                    if k == 0 and evac_wait is not None:
                        pe.wait_ge(evac, evac_wait + (j + 1))
                    m, n = j // 2, j % 2
                    for p, (a, b) in enumerate(AB):
                        ins = pe.matmul(bank[j][:, :], fT[a][:, k, m * P:(m + 1) * P],
                                        wS[b][:, slot, n * H:(n + 1) * H],
                                        start=(k == 0 and p == 0), stop=(k == K - 1 and p == 2))
                    if k == K - 1 and j != banks[-1]:
                        ins.then_inc(bank_done, 1)
                ins.then_inc(chunk_used, 1)

            ALL = range(8)
            for k in range(K):
                chunk(k, k, k % 4, ALL, None, first=True)
            with pe.Fori(1, UNITS) as u:
                for k in range(K):
                    chunk(u * K + k, k, k % 4, ALL, u * 8 - 8)
            for k in range(K):
                chunk(C_TOP + k, k, k % 4, range(2, 8), 8 * UNITS - 8)
            for k in range(K):
                chunk(C_TOP + K + k, k, k % 4, range(2), 8 * UNITS - 8)

            def transpose_edges(side):
                for r in range(TILE_HH):
                    pe.wait_ge(hh_in[r], 16 * (side + 1))
                for g in range(K // 2):
                    if side == 0:
                        pe.wait_ge(evac, 8 * UNITS + g + 3)
                    else:
                        pe.wait_ge(hh_lo_done, g + 1)
                    for i in range(2):
                        for r in range(TILE_HH):
                            f = 2 * g + i
                            ins = pe.transpose(bank[4 + g][:, (2 * i + r) * P:(2 * i + r + 1) * P],
                                               h_edge[:, r, f * P:(f + 1) * P], ident[:, :])
                    ins.then_inc(hhT_ready, 1)

            transpose_edges(0)
            pe.wait_ge(evac, 8 * UNITS + 8)
            for k in range(2 * K):
                if k == K - 2:
                    transpose_edges(1)
                side = k // K
                pe.wait_ge(hh_lo_done, side * (K // 2) + (k % K) // 2 + 1)
                pe.wait_ge(lo_done, C_HH + k + 1)
                for j in range(2 * TILE_HH):
                    r, n = j // 2, j % 2
                    for p, (a, b) in enumerate(AB):
                        ins = pe.matmul(bank[j][:, :], fT[a][:, k % K, (2 * side + r) * P:(2 * side + r + 1) * P],
                                        wS[b][:, k % 4, n * H:(n + 1) * H],
                                        start=(k == 0 and p == 0), stop=(k == 2 * K - 1 and p == 2))
                    if k == 2 * K - 1 and j < 2 * TILE_HH - 1:
                        ins.then_inc(bank_done, 1)
                ins.then_inc(chunk_used, 1)

            def adj_clear():
                for b in range(B):
                    pe.matmul(bank[b][:, :], zeros[:, :], node_no[:, :], start=True, stop=True)
                pe.matmul(bank[4][:, 0:4 * B], zeros[:, :], node_no[:, 0:4 * B], start=True, stop=True)

            def adj_close(deg):
                if deg:
                    pe.matmul(bank[4][:, 0:4 * B], zeros[:, :], node_no[:, 0:4 * B], start=False, stop=True,
                              skip_group_check=True)
                for b in range(B):
                    ins = pe.matmul(bank[b][:, :], zeros[:, :], node_no[:, :], start=False, stop=True,
                                    skip_group_check=True)
                ins.then_inc(adj_full, 1)

            def adj_sum(first_pair, deg):
                for pair in range(T // 2):
                    k, slot = pair % 4, pair % RING
                    word = words[pair // 4]
                    lo, hi = pe.snap((word >> (4 * k)) & 3), pe.snap((word >> (4 * k + 2)) & 3)
                    pe.wait_ge(dst_picked, first_pair + pair + 1)
                    pe.wait_ge(src_picked, first_pair + pair + 1)
                    if not deg:
                        pe.wait_ge(src0_picked, pair + 1)
                    if deg:
                        for r in range(2):
                            for b in range(B):
                                pe.matmul(bank[4][:, 4 * b:4 * b + 4], pick_src[slot][:, r, b * P:(b + 1) * P],
                                          w_col[:, 2 * pair + r, :], start=False, stop=True, skip_group_check=True)
                    with pe.Fori(lo, hi + 1) as b:
                        for r in range(2):
                            for p in range(3):
                                pe.matmul(banks[:, bass.ds(b * H, H)], pick_dst[slot][:, r, p, bass.ds(b * P, P)],
                                          pick_src[slot][:, r, :], start=False, stop=True, skip_group_check=True)
                    pe.matmul(bank[4][:, 0:B], zeros[:, :], node_no[:, 0:B], start=False, stop=True,
                              skip_group_check=True).then_inc(adj_done, 1)

            def transpose_adj(n):
                for b in range(B):
                    pe.wait_ge(adj_ready, n + b + 1)
                for s in range(B):
                    for b in range(B):
                        ins = pe.transpose(bank[4 + s][:, b * P:(b + 1) * P], adj[:, b, s * P:(s + 1) * P], ident[:, :])
                    ins.then_inc(adjT_done, 1)

            words = [pe.value_load(pair_word[0:1, q:q + 1], min_val=0, max_val=16 ** 4 - 1) for q in range(T // 8)]
            pe.wait_ge(hh_logits, TILE_HH)
            pe.wait_ge(hh_lo_done, K)
            adj_clear()
            adj_sum(0, True)
            adj_close(True)
            pe.wait_ge(mpart_ready, 1)
            for t in range(T):
                for b in range(B):
                    ins = pe.matmul(bank[5][:, 3 * t:3 * t + 3], member[:, b, t * P:(t + 1) * P], mpart[:, b, :],
                                    start=(b == 0), stop=(b == B - 1))
            ins.then_inc(me_done, 1)
            pe.wait_ge(arg_ready, 1)
            pe.wait_ge(wdeg_ready, 1)
            transpose_adj(0)
            pe.wait_ge(adjwT_ready, B)
            adj_clear()
            adj_sum(T // 2, False)
            adj_close(False)
            transpose_adj(B)

            def features(order, n_adj, n_hn, first_layer):
                for i, s in enumerate(order):
                    pe.wait_ge(adjT_lo_done, n_adj + (s + 1 if i == 0 or n_adj == 0 else B))
                    pe.wait_ge(hn_lo_done, n_hn + i + 1)
                    for f in range(K):
                        if i == 0 and first_layer and f >= 4:
                            pe.wait_ge(adjT_lo_done, f - 3)
                        if i == 0 and not first_layer:
                            pe.wait_ge(x2_step, f + 1)
                        for p, (a, b) in enumerate(AB):
                            ins = pe.matmul(bank[f][:, :], hn[a][:, s, f * P:(f + 1) * P], adjT[b][:, s, :],
                                            start=(i == 0 and p == 0), stop=(i == B - 1 and p == 2))
                        if i == B - 1:
                            ins.then_inc(z_done, 1)

            def products(c0, blocks):
                banks = range(2 * blocks[0], 2 * blocks[-1] + 2)
                for k in range(K // 2):
                    chunk(c0 + k, k, k % 4, banks, None)
                for m in blocks:
                    for k in range(K // 2, K):
                        if m == blocks[0]:
                            pe.wait_ge(lo_done, c0 + k + 1)
                        for n in range(2):
                            for p, (a, b) in enumerate(AB):
                                ins = pe.matmul(bank[2 * m + n][:, :], fT[a][:, k, m * P:(m + 1) * P],
                                                wS[b][:, k % 4, n * H:(n + 1) * H],
                                                start=False, stop=(k == K - 1 and p == 2))
                            if k == K - 1 and 2 * m + n != banks[-1]:
                                ins.then_inc(bank_done, 1)
                        if m == blocks[-1]:
                            ins.then_inc(chunk_used, 1)

            features(range(B), 0, 0, True)
            pe.wait_ge(fT_lo_done, 2 * K)
            for k in range(K):
                chunk(C_BOT + k, k, k % 4, range(2), None)
            products(C_BOT + K, range(BLOCK_H, B))
            pe.wait_ge(adjT_lo_done, 2 * B)
            features(range(B), B, B, False)
            pe.wait_ge(fT_lo_done, 3 * K)
            products(C_L1, range(B))


_INS = ["x", "src", "dst", "edge_weight", "L0_gnn_W_hh", "L0_gnn_b_hh", "L0_gnn_W_oo", "L0_gnn_b_oo", "L0_gnn_W_ho",
        "L0_gnn_b_ho", "L0_gnn_W_a", "L0_gnn_b_a", "L0_gnn_W_hn", "L0_gnn_b_hn", "L0_gnn_W_on", "L0_gnn_b_on",
        "L1_gnn_W", "L1_gnn_b"]


def kernel(**inputs):
    import numpy as _np
    import concourse.bacc as _bacc
    from concourse import mybir as _mybir
    from concourse.bass_utils import run_bass_kernel_spmd as _run

    nc = _bacc.Bacc("TRN2", target_bir_lowering=False, num_devices=1)
    arrays, args = {}, []
    for name in _INS:
        a = _np.ascontiguousarray(inputs[name])
        arrays[f"in_{name}_dram"] = a
        args.append(nc.dram_tensor(f"in_{name}_dram", a.shape, _mybir.dt.from_np(a.dtype), kind="ExternalInput").ap())
    out = nc.dram_tensor("out_0_dram", inputs["x"].shape, _mybir.dt.float32, kind="ExternalOutput").ap()
    build(nc, *args, out)
    r = _run(nc, [arrays], core_ids=[0])
    return r.results[0]["out_0_dram"]
```
